# Optimizing a Trainium2 kernel written in Bass

```python
import numpy as np
import jax
import jax.numpy as jnp

def _softmax(x, axis=-1):
    return jax.nn.softmax(x, axis=axis)

def _gelu(x):
    return jax.nn.gelu(x, approximate=True)

def _silu(x):
    return jax.nn.silu(x)

def _sigmoid(x):
    return jax.nn.sigmoid(x)

def _layernorm(x, axis=-1, eps=1e-05):
    m = jnp.mean(x, axis=axis, keepdims=True)
    v = jnp.var(x, axis=axis, keepdims=True)
    return (x - m) / jnp.sqrt(v + eps)

def _scatter_add(tgt, idx, src, axis=0):
    return tgt.at[idx].add(src)

def _segment_sum(src, seg, n):
    return jax.ops.segment_sum(src, seg, n)
kernel_name = 'mk_adj_preln_d4_adj_r2_c26fc5'

def setup_inputs(seed: int=0):
    np.random.seed(seed)
    _w = jnp.asarray

    def _rec_inputs():
        import jax
        import jax.numpy as jnp
        _gk = jax.random.key(seed)
        x = 7.22e-05 + 1 * jax.random.normal(jax.random.fold_in(_gk, 1), (32, 256, 128), jnp.float32)
        _a = jax.random.bernoulli(jax.random.fold_in(_gk, 2), 0.03125, (256, 256))
        _a = jnp.logical_or(_a, jnp.swapaxes(_a, -1, -2))
        _a = jnp.logical_or(_a, jnp.eye(256, dtype=bool))
        _af = _a.astype(jnp.float32)
        _af = _af * jax.random.uniform(jax.random.fold_in(_gk, 3), (256, 256), jnp.float32, 0.05, 0.000976562)
        adj = _af
        return (x, adj)
    x, adj = _rec_inputs()

    def _L0_gnn_setup():
        import jax, jax.numpy as jnp
        import numpy as np
        B, N, F_IN, F_OUT, ORDERS = (32, 1024, 128, 128, 2)
        NUM_MATRICES = 2 * ORDERS + 1

        def _cheb_hops(x0, A, orders):
            hops = []
            x1 = jnp.einsum('bnf,nw->bwf', x0, A)
            hops.append(x1)
            xk_1, xk_2 = (x1, x0)
            for _ in range(2, orders + 1):
                x2 = 2.0 * jnp.einsum('bnf,nw->bwf', xk_1, A) - xk_2
                hops.append(x2)
                xk_1, xk_2 = (x2, xk_1)
            return hops
        key = jax.random.key(seed)
        k1, k2, k3, k4, k5 = jax.random.split(key, 5)
        X = jax.random.normal(k1, (B, N, F_IN), dtype=jnp.float32)
        A1 = jax.random.uniform(k2, (N, N), dtype=jnp.float32) * (2.0 / N)
        A2 = jax.random.uniform(k3, (N, N), dtype=jnp.float32) * (2.0 / N)
        stdv = 1.0 / np.sqrt(F_OUT)
        Theta1 = jax.random.uniform(k4, (F_IN * NUM_MATRICES, F_OUT), dtype=jnp.float32, minval=-stdv, maxval=stdv)
        bias = jax.random.uniform(k5, (F_OUT,), dtype=jnp.float32, minval=-stdv, maxval=stdv)
        return {'X': X, 'A1': A1, 'A2': A2, 'Theta1': Theta1, 'bias': bias}
    _L0_gnn_all = _L0_gnn_setup()
    _L0_gnn_in = {k: v for k, v in _L0_gnn_all.items() if k in ('Theta1', 'bias')}
    del _L0_gnn_all

    def _L1_gnn_setup():
        import jax, jax.numpy as jnp
        import numpy as np
        B, N, D = (32, 512, 128)
        TIME_STEP = 5
        key = jax.random.key(seed)
        ks = jax.random.split(key, 12)
        s2 = 1.0 / np.sqrt(2 * D)
        s1 = 1.0 / np.sqrt(D)
        return {'input': jax.random.normal(ks[0], (B, N, D), jnp.float32), 'in_matrix': jax.random.uniform(ks[1], (N, N), jnp.float32), 'out_matrix': jax.random.uniform(ks[2], (N, N), jnp.float32), 'w3_w': jax.random.normal(ks[3], (D, 2 * D), jnp.float32) * s2, 'w3_b': jnp.zeros((D,), jnp.float32), 'u3_w': jax.random.normal(ks[4], (D, D), jnp.float32) * s1, 'u3_b': jnp.zeros((D,), jnp.float32), 'w4_w': jax.random.normal(ks[5], (D, 2 * D), jnp.float32) * s2, 'w4_b': jnp.zeros((D,), jnp.float32), 'w5_w': jax.random.normal(ks[6], (D, 2 * D), jnp.float32) * s2, 'w5_b': jnp.zeros((D,), jnp.float32), 'u5_w': jax.random.normal(ks[7], (D, D), jnp.float32) * s1, 'u5_b': jnp.zeros((D,), jnp.float32), 'time_step': TIME_STEP}
    _L1_gnn_all = _L1_gnn_setup()
    _L1_gnn_in = {k: v for k, v in _L1_gnn_all.items() if k in ('w3_w', 'w3_b', 'u3_w', 'u3_b', 'w4_w', 'w4_b', 'w5_w', 'w5_b', 'u5_w', 'u5_b')}
    del _L1_gnn_all

    def _L2_gnn_setup():
        import jax, jax.numpy as jnp
        import numpy as np
        B, N, D = (32, 512, 128)
        LEAKY_ALPHA = 0.2
        LN_EPS = 1e-14
        key = jax.random.key(seed)
        k1, k2 = jax.random.split(key)
        x = jax.random.normal(k1, (B, N, D), dtype=jnp.float32)
        limit = 1.414 * np.sqrt(6.0 / (2 * D + 1))
        a = jax.random.uniform(k2, (2 * D, 1), dtype=jnp.float32, minval=-limit, maxval=limit)
        gamma = jnp.ones((N, N), dtype=jnp.float32)
        beta = jnp.zeros((N, N), dtype=jnp.float32)
        return {'x': x, 'a': a, 'gamma': gamma, 'beta': beta}
    _L2_gnn_all = _L2_gnn_setup()
    _L2_gnn_in = {k: v for k, v in _L2_gnn_all.items() if k in ('a',)}
    del _L2_gnn_all

    def _L3_gnn_setup():
        import jax, jax.numpy as jnp
        import numpy as np
        from jax import lax
        CONV_ORDER = 3

        def _chebyshev(adj, x, order):

            def step(carry, _):
                nxt = jnp.einsum('ij,bjc->bic', adj, carry)
                return (nxt, nxt)
            _, xs = lax.scan(step, x, None, length=order)
            return jnp.moveaxis(xs, 0, -1)
        key = jax.random.key(seed)
        k1, k2, k3, k4 = jax.random.split(key, 4)
        B, E, C_in, C_out, K, n_adjs = (8, 2048, 128, 128, CONV_ORDER, 2)
        x_1 = jax.random.normal(k1, (B, E, C_in), dtype=jnp.float32)
        adj0 = jax.random.normal(k2, (E, E), dtype=jnp.float32) / np.sqrt(E)
        adj1 = jax.random.normal(k3, (E, E), dtype=jnp.float32) / np.sqrt(E)
        kdim = K * n_adjs + 1
        std = 1.414 * np.sqrt(2.0 / float((C_in + C_out) * kdim))
        weight_1 = std * jax.random.normal(k4, (C_in, C_out, kdim), dtype=jnp.float32)
        return {'x_1': x_1, 'adj0': adj0, 'adj1': adj1, 'weight_1': weight_1}
    _L3_gnn_all = _L3_gnn_setup()
    _L3_gnn_in = {k: v for k, v in _L3_gnn_all.items() if k in ('weight_1',)}
    del _L3_gnn_all
    return {'x': x, 'adj': adj, 'L0_gnn_Theta1': _L0_gnn_in['Theta1'], 'L0_gnn_bias': _L0_gnn_in['bias'], 'L1_gnn_w3_w': _L1_gnn_in['w3_w'], 'L1_gnn_w3_b': _L1_gnn_in['w3_b'], 'L1_gnn_u3_w': _L1_gnn_in['u3_w'], 'L1_gnn_u3_b': _L1_gnn_in['u3_b'], 'L1_gnn_w4_w': _L1_gnn_in['w4_w'], 'L1_gnn_w4_b': _L1_gnn_in['w4_b'], 'L1_gnn_w5_w': _L1_gnn_in['w5_w'], 'L1_gnn_w5_b': _L1_gnn_in['w5_b'], 'L1_gnn_u5_w': _L1_gnn_in['u5_w'], 'L1_gnn_u5_b': _L1_gnn_in['u5_b'], 'L2_gnn_a': _L2_gnn_in['a'], 'L3_gnn_weight_1': _L3_gnn_in['weight_1']}

def reference(x, adj, L0_gnn_Theta1, L0_gnn_bias, L1_gnn_w3_w, L1_gnn_w3_b, L1_gnn_u3_w, L1_gnn_u3_b, L1_gnn_w4_w, L1_gnn_w4_b, L1_gnn_w5_w, L1_gnn_w5_b, L1_gnn_u5_w, L1_gnn_u5_b, L2_gnn_a, L3_gnn_weight_1):
    import jax
    import jax.numpy as jnp

    def _L0_gnn_ref(X, A1, A2, Theta1, bias):
        import jax, jax.numpy as jnp
        import numpy as np
        B, N, F_IN, F_OUT, ORDERS = (32, 1024, 128, 128, 2)
        NUM_MATRICES = 2 * ORDERS + 1

        def _cheb_hops(x0, A, orders):
            hops = []
            x1 = jnp.einsum('bnf,nw->bwf', x0, A)
            hops.append(x1)
            xk_1, xk_2 = (x1, x0)
            for _ in range(2, orders + 1):
                x2 = 2.0 * jnp.einsum('bnf,nw->bwf', xk_1, A) - xk_2
                hops.append(x2)
                xk_1, xk_2 = (x2, xk_1)
            return hops
        xs = [X] + _cheb_hops(X, A1, ORDERS) + _cheb_hops(X, A2, ORDERS)
        x = jnp.stack(xs, axis=2)
        b, n = (X.shape[0], X.shape[1])
        x = x.reshape(b, n, -1)
        out = jax.nn.relu(x @ Theta1 + bias)
        return out

    def _L1_gnn_ref(input, in_matrix, out_matrix, w3_w, w3_b, u3_w, u3_b, w4_w, w4_b, w5_w, w5_b, u5_w, u5_b, time_step):
        import jax, jax.numpy as jnp
        import numpy as np
        B, N, D = (32, 512, 128)
        TIME_STEP = 5

        def step(h, _):
            m_in = jnp.einsum('nm,bmd->bnd', in_matrix, h)
            m_out = jnp.einsum('nm,bmd->bnd', out_matrix, h)
            av = jnp.concatenate([m_in, m_out], axis=-1)
            u3 = h @ u3_w.T + u3_b
            z = jax.nn.sigmoid(av @ w3_w.T + w3_b + u3)
            r = jax.nn.sigmoid(av @ w4_w.T + w4_b + u3)
            hv = jnp.tanh(av @ w5_w.T + w5_b + (r * h @ u5_w.T + u5_b))
            h = (1.0 - z) * h + z * hv
            return (h, None)
        h, _ = jax.lax.scan(step, input, None, length=time_step)
        return h

    def _L2_gnn_ref(x, a, gamma, beta):
        import jax, jax.numpy as jnp
        import numpy as np
        B, N, D = (32, 512, 128)
        LEAKY_ALPHA = 0.2
        LN_EPS = 1e-14
        d = x.shape[-1]
        a_i = a[:d, 0]
        a_j = a[d:, 0]
        e = (x @ a_i)[:, :, None] + (x @ a_j)[:, None, :]
        mean = jnp.mean(e, axis=(1, 2), keepdims=True)
        var = jnp.mean(jnp.square(e - mean), axis=(1, 2), keepdims=True)
        e = (e - mean) * jax.lax.rsqrt(var + LN_EPS) * gamma + beta
        e = jnp.where(e >= 0, e, LEAKY_ALPHA * e)
        alpha = jax.nn.softmax(e, axis=1)
        h = jax.nn.sigmoid(jnp.einsum('bij,bjd->bid', alpha, x))
        return h

    def _L3_gnn_ref(x_1, adj0, adj1, weight_1):
        import jax, jax.numpy as jnp
        import numpy as np
        from jax import lax
        CONV_ORDER = 3

        def _chebyshev(adj, x, order):

            def step(carry, _):
                nxt = jnp.einsum('ij,bjc->bic', adj, carry)
                return (nxt, nxt)
            _, xs = lax.scan(step, x, None, length=order)
            return jnp.moveaxis(xs, 0, -1)
        parts = [x_1[..., None], _chebyshev(adj0, x_1, CONV_ORDER), _chebyshev(adj1, x_1, CONV_ORDER)]
        x_all = jnp.concatenate(parts, axis=3)
        y_1 = jnp.einsum('bnik,iok->bno', x_all, weight_1)
        return y_1
    h = jnp.maximum(_layernorm(x, axis=-1), 0.0)
    x = x + _L0_gnn_ref(h, adj, adj, L0_gnn_Theta1, L0_gnn_bias)
    h = jnp.maximum(_layernorm(x, axis=-1), 0.0)
    x = x + _L1_gnn_ref(h, adj, adj, L1_gnn_w3_w, L1_gnn_w3_b, L1_gnn_u3_w, L1_gnn_u3_b, L1_gnn_w4_w, L1_gnn_w4_b, L1_gnn_w5_w, L1_gnn_w5_b, L1_gnn_u5_w, L1_gnn_u5_b, 5)
    h = jnp.maximum(_layernorm(x, axis=-1), 0.0)
    x = x + _L2_gnn_ref(h, L2_gnn_a, adj, adj)
    h = jnp.maximum(_layernorm(x, axis=-1), 0.0)
    x = x + _L3_gnn_ref(h, adj, adj, L3_gnn_weight_1)
    return x

_drawn_inputs = setup_inputs


def setup_inputs(seed=0):
    import zlib

    import numpy as np

    out = dict(_drawn_inputs(seed))
    spreads = {'L1_gnn_w3_b': (0.0, 0.773),
     'L1_gnn_u3_b': (0.0, 0.527),
     'L1_gnn_w4_b': (0.0, 2.0),
     'L1_gnn_w5_b': (0.0, 0.1),
     'L1_gnn_u5_b': (0.0, 0.1)}
    factors = {'L1_gnn_w4_w': 4.563, 'L2_gnn_a': 64.0}
    for name, (base, spread) in spreads.items():
        noise = np.random.default_rng([zlib.crc32(name.encode()), seed]).standard_normal(out[name].shape)
        drawn = base * np.exp(spread * noise) if base else spread * noise
        out[name] = jnp.asarray(drawn.astype(out[name].dtype))
    for name, factor in factors.items():
        out[name] = (out[name] * factor).astype(out[name].dtype)
    return out
```

```python
from contextlib import ExitStack

import concourse.bass as bass
from concourse import mybir

F32 = mybir.dt.float32
F32R = mybir.dt.float32r
ALU = mybir.AluOpType
ACT = mybir.ActivationFunctionType
AX = mybir.AxisListType

P = 128
B, N, D = 32, 256, 128
NT = N // P
GB = 2
G = B // GB
NK = NT * GB
W = GB * N
STEPS = 5
ITEMS = STEPS * G
LN_EPS = 1e-5
ATT_EPS = 1e-14
LEAK = 0.2
MINUS_HALF, HALF, QUARTER, EPS = range(4)


class Item:

    def __init__(self, q, r, unroll, items):
        self.q, self.r, self.u, self.items = q, r, unroll, items

    def count(self, ago=0, per=1):
        at = per * (self.r - ago + 1)
        if isinstance(self.q, int):
            return min(per * self.u * self.q + at, per * self.items)
        return self.q * (per * self.u) + at

    def dma(self, per=1):
        return self.q * (16 * per) + 16 * per

    def index(self):
        return self.q * self.u + self.r


def place(eng, index):
    return index if isinstance(index, int) else eng.snap(index)


def wait(eng, sem, value):
    if not isinstance(value, int) or value > 0:
        eng.wait_ge(sem, value)


def sweep(eng, items, unroll, head, lag, body):
    def slot(q, j, bounded):
        def stage(behind):
            r = j - behind
            q_, r_ = q + r // unroll if r // unroll else q, r % unroll
            if bounded and not 0 <= unroll * q_ + r_ < items:
                return None
            return Item(q_, r_, unroll, items)
        body(stage)

    for q in range(head):
        for j in range(unroll):
            slot(q, j, True)
    with eng.Fori(head, items // unroll, 1) as q:
        for j in range(unroll):
            slot(q, j, False)
    for s in range(items, items + lag):
        slot(s // unroll, s % unroll, True)


def build(nc, x, adj, Theta1, bias0, w3_w, w3_b, u3_w, u3_b, w4_w, w4_b, w5_w, w5_b, u5_w, u5_b, att, weight_1, out):
    x_dram = x.rearrange("b (t p) f -> b p t f", p=P)
    out_dram = out.rearrange("b (t p) f -> b p t f", p=P)

    with ExitStack() as whole:
        def sb(name, shape, dt=F32, ctx=whole):
            return ctx.enter_context(nc.sbuf_tensor(name, shape, dt))

        def sem(name):
            return whole.enter_context(nc.semaphore(name))

        psum = whole.enter_context(nc.psum_tensor("psum", [P, 8, 512], F32))

        x_store = sb("x_store", [P, G, W])
        h_store = sb("h_store", [P, G, W])

        ident = sb("ident", [P, P])
        adj_nat = sb("adj_nat", [P, NT, N])
        adj_tr = sb("adj_tr", [P, NT, N])
        adj_nat_hi, adj_nat_lo = sb("adj_nat_hi", [P, NT, N], F32R), sb("adj_nat_lo", [P, NT, N], F32R)
        adj_tr_hi, adj_tr_lo = sb("adj_tr_hi", [P, NT, N], F32R), sb("adj_tr_lo", [P, NT, N], F32R)
        cheb0 = sb("cheb0", [P, 3, P])
        cheb3 = sb("cheb3", [P, 4, P])
        gate_w = sb("gate_w", [P, 5, P])
        gate_hi, gate_lo = sb("gate_hi", [P, 5, P], F32R), sb("gate_lo", [P, 5, P], F32R)
        gate_b = sb("gate_b", [P, 3])
        ones_hi = sb("ones_hi", [1, P], F32R)
        bias_row = sb("bias_row", [1, W])
        bias_hi, bias_lo = sb("bias_hi", [1, W], F32R), sb("bias_lo", [1, W], F32R)
        att_col = sb("att_col", [P, 2])
        att_rep = sb("att_rep", [P, 2, P])
        consts = sb("consts", [P, 4, NK])
        ones = sb("ones", [P, W])

        x_in_landed = [sem(f"x_in_landed{r}") for r in range(4)]
        x_stored = [sem(f"x_stored{r}") for r in range(4)]
        h_stored = [sem(f"h_stored{r}") for r in range(4)]

        prepare(nc, psum, sem, sb, ident, adj, adj_nat, adj_tr, adj_nat_hi, adj_nat_lo, adj_tr_hi, adj_tr_lo,
                Theta1, cheb0, weight_1, cheb3, (w3_w, w4_w, w5_w, u3_w, u5_w), gate_w, gate_hi, gate_lo,
                (w3_b, w4_b, w5_b, u3_b, u5_b), gate_b, bias0, ones_hi, bias_row, bias_hi, bias_lo,
                att, att_col, att_rep, consts, ones)
        layer0(nc, psum, sem, x_dram, x_store, h_store, x_in_landed, x_stored, h_stored, ident,
               adj_nat_hi, adj_nat_lo, cheb0, ones_hi, bias_hi, bias_lo, consts)
        layer1(nc, psum, sem, h_store, h_stored, ident, adj_tr_hi, adj_tr_lo, gate_hi, gate_lo, gate_b)
        layers23(nc, psum, sem, x_store, h_store, out_dram, ident, adj_tr, adj_tr_hi, adj_tr_lo, cheb3,
                 att_col, att_rep, consts, ones)


def prepare(nc, psum, sem, sb, ident, adj, adj_nat, adj_tr, adj_nat_hi, adj_nat_lo, adj_tr_hi, adj_tr_lo,
            Theta1, cheb0, weight_1, cheb3, weights, gate_w, gate_hi, gate_lo,
            biases, gate_b, bias0, ones_hi, bias_row, bias_hi, bias_lo, att, att_col, att_rep, consts, ones):
    w3_w, w4_w, w5_w, u3_w, u5_w = weights
    with ExitStack() as ctx:
        theta = sb("theta", [P, 5, P], F32, ctx)
        cheb_raw = sb("cheb_raw", [P, P, 7], F32, ctx)
        gate_raw = sb("gate_raw", [P, 8, P], F32, ctx)
        gate_sum = sb("gate_sum", [P, 5, P], F32, ctx)
        bias_raw = sb("bias_raw", [P, 5], F32, ctx)
        loaded, adj_loaded = sem("loaded"), sem("adj_loaded")
        zeroed, ident_set, consts_set, ones_set = sem("zeroed"), sem("ident_set"), sem("consts_set"), sem("ones_set")
        adj_turned, adj_tr_set, adj_split, adj_hi_set = sem("adj_turned"), sem("adj_tr_set"), sem("adj_split"), sem("adj_hi_set")
        summed, turned, gate_set, gate_hi_set, w34 = sem("summed"), sem("turned"), sem("gate_set"), sem("gate_hi_set"), sem("w34")
        cheb_part, row_hi = sem("cheb_part"), sem("row_hi")
        LOADS = 16 * (7 + 5 + NK + 2)
        with nc.Block() as block:
            @block.sync
            def _(sp):
                sp.dma_start(adj_nat[:], adj.rearrange("(t p) w -> p t w", p=P)).then_inc(adj_loaded, 16)
                sp.dma_start(gate_raw[:, 0:2, :], w4_w.rearrange("o (c i) -> o c i", i=P)).then_inc(loaded, 16)
                sp.dma_start(gate_raw[:, 2:4, :], w3_w.rearrange("o (c i) -> o c i", i=P)).then_inc(loaded, 16)
                sp.dma_start(gate_raw[:, 4:6, :], w5_w.rearrange("o (c i) -> o c i", i=P)).then_inc(loaded, 16)
                sp.dma_start(gate_raw[:, 6, :], u3_w).then_inc(loaded, 16)
                sp.dma_start(gate_raw[:, 7, :], u5_w).then_inc(loaded, 16)
                sp.dma_start(theta[:], Theta1.rearrange("(k f) o -> f k o", f=P)).then_inc(loaded, 16)
                sp.dma_start(cheb_raw[:], weight_1).then_inc(loaded, 16)
                for k, b in enumerate(biases):
                    sp.dma_start(bias_raw[:, k:k + 1], b.rearrange("(p o) -> p o", o=1)).then_inc(loaded, 16)
                for k in range(NK):
                    sp.dma_start(bias_row[:, k * P:(k + 1) * P], bias0.rearrange("(o f) -> o f", o=1)).then_inc(loaded, 16)
                for k in range(2):
                    sp.dma_start(att_col[:, k:k + 1], att[k * D:(k + 1) * D, :]).then_inc(loaded, 16)


            @block.gpsimd
            def _(pool):
                nc.gpsimd.memset(ident[:], 0.0).then_inc(zeroed, 1)
                pool.wait_ge(zeroed, 1)
                nc.gpsimd.affine_select(out=ident[:], in_=ident[:], compare_op=ALU.not_equal, fill=1.0, base=0,
                                        pattern=[[-1, P]], channel_multiplier=1).then_inc(ident_set, 1)
                for which, value in ((MINUS_HALF, -0.5), (HALF, 0.5), (QUARTER, 0.25), (EPS, ATT_EPS)):
                    nc.gpsimd.memset(consts[:, which], value).then_inc(consts_set, 1)

            @block.vector
            def _(dve):
                nc.vector.memset(ones[:], 1.0).then_inc(ones_set, 1)
                dve.wait_ge(adj_loaded, 16)
                dve.wait_ge(adj_hi_set, 1)
                nc.vector.tensor_tensor(adj_nat_lo[:], adj_nat[:], adj_nat_hi[:].bitcast(F32), ALU.subtract).then_inc(adj_split, 1)
                dve.wait_ge(adj_turned, 1)
                nc.vector.tensor_copy(adj_tr[:].rearrange("p t n -> p (t n)"), psum[:, 0, :]).then_inc(adj_tr_set, 1)
                dve.wait_ge(adj_hi_set, 2)
                dve.wait_ge(adj_tr_set, 1)
                nc.vector.tensor_tensor(adj_tr_lo[:], adj_tr[:], adj_tr_hi[:].bitcast(F32), ALU.subtract).then_inc(adj_split, 1)
                dve.wait_ge(loaded, LOADS)
                halves = gate_raw[:, 0:6, :].rearrange("p (k c) i -> p k c i", c=2)
                nc.vector.tensor_tensor(gate_sum[:, 0:3, :], halves[:, :, 0, :], halves[:, :, 1, :], ALU.add).then_inc(summed, 1)
                nc.vector.tensor_copy(gate_sum[:, 3:5, :], gate_raw[:, 6:8, :]).then_inc(summed, 1)
                nc.vector.tensor_tensor(cheb0[:, 1, :], theta[:, 1, :], theta[:, 3, :], ALU.add).then_inc(cheb_part, 1)
                nc.vector.tensor_tensor(cheb0[:, 2, :], theta[:, 2, :], theta[:, 4, :], ALU.add).then_inc(cheb_part, 1)
                dve.wait_ge(cheb_part, 2)
                nc.vector.tensor_tensor(cheb0[:, 0, :], theta[:, 0, :], cheb0[:, 2, :], ALU.subtract).then_inc(cheb_part, 1)
                dve.wait_ge(cheb_part, 3)
                nc.vector.tensor_scalar(cheb0[:, 2, :], cheb0[:, 2, :], 2.0, None, ALU.mult).then_inc(cheb_part, 1)
                nc.vector.tensor_copy(cheb3[:, 0, :], cheb_raw[:, :, 0]).then_inc(cheb_part, 1)
                for k in range(1, 4):
                    nc.vector.tensor_tensor(cheb3[:, k, :], cheb_raw[:, :, k], cheb_raw[:, :, k + 3], ALU.add).then_inc(cheb_part, 1)
                for k, other in ((0, 1), (1, 0), (2, 2)):
                    nc.vector.tensor_tensor(gate_b[:, k:k + 1], bias_raw[:, other:other + 1],
                                            bias_raw[:, 3 + k // 2:4 + k // 2], ALU.add).then_inc(cheb_part, 1)
                for k in range(2):
                    nc.vector.tensor_scalar(att_rep[:, k, :], ones[:, 0:P], att_col[:, k:k + 1], None, ALU.mult).then_inc(cheb_part, 1)
                nc.vector.tensor_copy(ones_hi[:], ones[0:1, 0:P]).then_inc(cheb_part, 1)
                dve.wait_ge(row_hi, 1)
                nc.vector.tensor_tensor(bias_lo[:], bias_row[:], bias_hi[:].bitcast(F32), ALU.subtract).then_inc(cheb_part, 1)
                dve.wait_ge(turned, 1)
                nc.vector.tensor_copy(gate_w[:, 0:4, :].rearrange("p k o -> p (k o)"), psum[:, 1, :]).then_inc(gate_set, 1)
                nc.vector.tensor_copy(gate_w[:, 4, :], psum[:, 2, 0:P]).then_inc(gate_set, 1)
                dve.wait_ge(gate_set, 2)
                nc.vector.tensor_tensor(gate_w[:, 1, :], gate_w[:, 1, :], gate_w[:, 0, :], ALU.subtract).then_inc(w34, 1)
                dve.wait_ge(gate_hi_set, 1)
                nc.vector.tensor_tensor(gate_lo[:], gate_w[:], gate_hi[:].bitcast(F32), ALU.subtract).then_inc(gate_set, 1)

            @block.scalar
            def _(act):
                act.wait_ge(adj_loaded, 16)
                nc.scalar.activation(adj_nat_hi[:], adj_nat[:], ACT.Copy).then_inc(adj_hi_set, 1)
                act.wait_ge(adj_tr_set, 1)
                nc.scalar.activation(adj_tr_hi[:], adj_tr[:], ACT.Copy).then_inc(adj_hi_set, 1)
                act.wait_ge(loaded, LOADS)
                nc.scalar.activation(bias_hi[:], bias_row[:], ACT.Copy).then_inc(row_hi, 1)
                act.wait_ge(w34, 1)
                nc.scalar.activation(gate_hi[:], gate_w[:], ACT.Copy).then_inc(gate_hi_set, 1)

            @block.tensor
            def _(pe):
                pe.wait_ge(ident_set, 1)
                pe.wait_ge(adj_loaded, 16)
                for t in range(NT):
                    for u in range(NT):
                        last = nc.tensor.transpose(psum[:, 0, (u * NT + t) * P:(u * NT + t + 1) * P],
                                                   adj_nat[:, t, u * P:(u + 1) * P], ident[:])
                last.then_inc(adj_turned, 1)
                pe.wait_ge(summed, 2)
                for k in range(5):
                    last = nc.tensor.transpose(psum[:, 1 + k // 4, (k % 4) * P:(k % 4 + 1) * P], gate_sum[:, k, :], ident[:])
                last.then_inc(turned, 1)


def norm_sems(sem, name):
    return {k: sem(f"{name}_{k}") for k in ("stats", "sums", "scaled", "quarter", "var", "rstd")}


def norm_stats(dve, s, stats, tile, width):
    for k in range(NK):
        last = dve.bn_stats(stats[:, k, :], tile[:, k * width:(k + 1) * width])
    last.then_inc(s["stats"], 1)


def variance(pool, s, item, stats, work, mean, count, eps, consts):
    mean_e, m2_e, mean_o, m2_o = (stats[:, :, k] for k in (1, 2, 4, 5))
    total, diff, dev, square = (work[:, k, :] for k in range(4))
    pool.wait_ge(s["stats"], item.count())
    pool.tensor_tensor(total, mean_e, mean_o, ALU.add).then_inc(s["sums"], 1)
    pool.tensor_tensor(diff, mean_e, mean_o, ALU.subtract).then_inc(s["sums"], 1)
    pool.tensor_tensor(dev, m2_e, m2_o, ALU.add).then_inc(s["sums"], 1)
    pool.wait_ge(s["sums"], item.count(per=3))
    pool.tensor_tensor(square, diff, diff, ALU.mult).then_inc(s["scaled"], 1)
    pool.tensor_scalar(mean, total, 0.5, 0.0, ALU.mult, ALU.add).then_inc(s["scaled"], 1)
    pool.tensor_scalar(dev, dev, 1.0 / count, eps, ALU.mult, ALU.add).then_inc(s["scaled"], 1)
    pool.wait_ge(s["scaled"], item.count(per=3))
    pool.tensor_tensor(square, square, consts[:, QUARTER], ALU.mult).then_inc(s["quarter"], 1)
    pool.wait_ge(s["quarter"], item.count())
    pool.tensor_tensor(dev, dev, square, ALU.add).then_inc(s["var"], 1)
    return dev


def norm_scalars(pool, s, item, stats, work, mean, rstd, consts):
    dev = variance(pool, s, item, stats, work, mean, D, LN_EPS, consts)
    pool.wait_ge(s["var"], item.count())
    pool.tensor_tensor(rstd, dev, consts[:, MINUS_HALF], ALU.pow).then_inc(s["rstd"], 1)


def normalise(dve, tile, source, mean, rstd, done):
    for k in range(NK):
        last = dve.tensor_scalar(tile[:, k * D:(k + 1) * D], source[:, k * D:(k + 1) * D],
                                 mean[:, k:k + 1], rstd[:, k:k + 1], ALU.subtract, ALU.mult)
    last.then_inc(done, 1)


def flip(pe, bank, tile, ident, done):
    for t in range(NT):
        for b in range(GB):
            k, c = t * GB + b, b * NT + t
            last = pe.transpose(bank[:, c * P:(c + 1) * P], tile[:, k * P:(k + 1) * P], ident[:])
    last.then_inc(done, 1)


def flip_back(pe, bank, tile, ident, done):
    for t in range(NT):
        for b in range(GB):
            k, c = t * GB + b, b * NT + t
            last = pe.transpose(bank[:, k * P:(k + 1) * P], tile[:, c * P:(c + 1) * P], ident[:])
    last.then_inc(done, 1)


def by_weight(pe, bank, h_feat, weight):
    for t in range(NT):
        for b in range(GB):
            k, c = t * GB + b, b * NT + t
            last = pe.matmul(bank[:, k * P:(k + 1) * P], h_feat[:, c * P:(c + 1) * P], weight,
                             start=(k == 0), stop=False, skip_group_check=True)
    return last


def by_adjacency(pe, bank, mat_hi, mat_lo, v_hi, v_lo):
    for n in range(NT):
        for m in range(NT):
            for left, right in ((mat_hi, v_hi), (mat_hi, v_lo), (mat_lo, v_hi)):
                last = pe.matmul(bank[:, n * GB * D:(n + 1) * GB * D], left[:, m, n * P:(n + 1) * P],
                                 right[:, m * GB * D:(m + 1) * GB * D], start=False, stop=False, skip_group_check=True)
    return last


def layer0(nc, psum, sem, x_dram, x_store, h_store, x_in_landed, x_stored, h_stored, ident,
           adj_hi, adj_lo, cheb0, ones_hi, bias_hi, bias_lo, consts):
    U = 4
    with ExitStack() as ctx:
        def ring(name, n, shape=(W,), dt=F32):
            t = ctx.enter_context(nc.sbuf_tensor("l0_" + name, [P, n, *shape], dt))
            return [t[:, k] for k in range(n)]

        x_in, x_new = ring("x_in", 4), ring("x_new", 4)
        y, y_new = ring("y", 2), ring("y_new", 2)
        h_feat, h_next = ring("h_feat", 2), ring("h_next", 4)
        v_hi, v_lo = ring("v_hi", 2, dt=F32R), ring("v_lo", 2, dt=F32R)
        u_hi, u_lo = ring("u_hi", 2, dt=F32R), ring("u_lo", 2, dt=F32R)
        stats, stats_new = ring("stats", 2, (NK, 6)), ring("stats_new", 2, (NK, 6))
        work, work_new = ring("work", 2, (4, NK)), ring("work_new", 2, (4, NK))
        mean, rstd = ring("mean", 2, (NK,)), ring("rstd", 2, (NK,))
        mean_new, rstd_new = ring("mean_new", 2, (NK,)), ring("rstd_new", 2, (NK,))
        n_in, n_out = norm_sems(sem, "l0_in"), norm_sems(sem, "l0_out")
        y_set, y_new_set = sem("l0_y_set"), sem("l0_y_new_set")
        turned, turned_new = sem("l0_turned"), sem("l0_turned_new")
        h_set, h_next_set = sem("l0_h_set"), sem("l0_h_next_set")
        v_sum, v_hi_set, v_lo_set = sem("l0_v_sum"), sem("l0_v_hi_set"), sem("l0_v_lo_set")
        u_sum, u_hi_set, u_lo_set = sem("l0_u_sum"), sem("l0_u_hi_set"), sem("l0_u_lo_set")
        o_sum, x_new_set = sem("l0_o_sum"), sem("l0_x_new_set")
        T_BANK, T_NEW_BANK, V_BANK, U_BANK, O_BANK = (psum[:, k] for k in (0, 1, 2, 3, 4))

        with nc.Block() as block:
            @block.sync
            def _(sp):
                def body(stage):
                    if i := stage(0):
                        at = place(sp, i.index())
                        wait(sp, x_new_set, i.count(4))
                        for b in range(GB):
                            sp.dma_start(x_in[i.r].rearrange("p (t b f) -> p b t f", t=NT, b=GB)[:, b],
                                         x_dram[at * GB + b]).then_inc(x_in_landed[i.r], 16)
                    if i := stage(7):
                        at = place(sp, i.index())
                        sp.wait_ge(x_new_set, i.count())
                        sp.wait_ge(h_next_set, i.count())
                        sp.dma_start(x_store[:, at], x_new[i.r]).then_inc(x_stored[i.r], 16)
                        sp.dma_start(h_store[:, at], h_next[i.r]).then_inc(h_stored[i.r], 16)
                sweep(sp, G, U, 2, 7, body)
                for k in range(U):
                    sp.wait_ge(x_stored[k], 16 * (G // U))
                for k in range(U):
                    sp.wait_ge(h_stored[k], 16 * (G // U))

            @block.gpsimd
            def _(pool):
                def body(stage):
                    if i := stage(0):
                        wait(pool, y_set, i.count(2))
                        norm_scalars(pool, n_in, i, stats[i.r % 2], work[i.r % 2], mean[i.r % 2], rstd[i.r % 2], consts)
                    if i := stage(3):
                        wait(pool, y_new_set, i.count(2))
                        norm_scalars(pool, n_out, i, stats_new[i.r % 2], work_new[i.r % 2], mean_new[i.r % 2],
                                     rstd_new[i.r % 2], consts)
                sweep(pool, G, U, 2, 3, body)

            @block.vector
            def _(dve):
                def body(stage):
                    if i := stage(0):
                        dve.wait_ge(x_in_landed[i.r], i.dma(per=GB))
                        wait(dve, n_in["sums"], i.count(2, per=3))
                        norm_stats(dve, n_in, stats[i.r % 2], x_in[i.r], D)
                    if i := stage(1):
                        dve.wait_ge(n_in["rstd"], i.count())
                        wait(dve, turned, i.count(2))
                        normalise(dve, y[i.r % 2], x_in[i.r], mean[i.r % 2], rstd[i.r % 2], y_set)
                    if i := stage(2):
                        dve.wait_ge(v_hi_set, i.count())
                        wait(dve, u_sum, i.count(2))
                        dve.tensor_tensor(v_lo[i.r % 2], V_BANK, v_hi[i.r % 2].bitcast(F32), ALU.subtract).then_inc(v_lo_set, 1)
                    if i := stage(3):
                        dve.wait_ge(o_sum, i.count())
                        if not isinstance(i.q, int) or i.q > 0:
                            dve.wait_ge(x_stored[i.r], i.q * 16)
                        dve.scalar_tensor_tensor(x_new[i.r], O_BANK, 0.0, x_in[i.r], ALU.max, ALU.add).then_inc(x_new_set, 1)
                        dve.wait_ge(x_new_set, i.count())
                        wait(dve, n_out["sums"], i.count(2, per=3))
                        norm_stats(dve, n_out, stats_new[i.r % 2], x_new[i.r], D)
                    if i := stage(4):
                        dve.wait_ge(n_out["rstd"], i.count())
                        wait(dve, turned_new, i.count(2))
                        normalise(dve, y_new[i.r % 2], x_new[i.r], mean_new[i.r % 2], rstd_new[i.r % 2], y_new_set)
                    if i := stage(2):
                        dve.wait_ge(u_hi_set, i.count())
                        wait(dve, o_sum, i.count(2))
                        dve.tensor_tensor(u_lo[i.r % 2], U_BANK, u_hi[i.r % 2].bitcast(F32), ALU.subtract).then_inc(u_lo_set, 1)
                sweep(dve, G, U, 2, 4, body)

            @block.scalar
            def _(act):
                def body(stage):
                    if i := stage(0):
                        act.wait_ge(turned, i.count())
                        wait(act, o_sum, i.count(2))
                        act.activation(h_feat[i.r % 2], T_BANK, ACT.Relu).then_inc(h_set, 1)
                    if i := stage(1):
                        act.wait_ge(u_sum, i.count())
                        wait(act, o_sum, i.count(2))
                        act.activation(u_hi[i.r % 2], U_BANK, ACT.Copy).then_inc(u_hi_set, 1)
                    if i := stage(0):
                        act.wait_ge(v_sum, i.count())
                        wait(act, u_sum, i.count(2))
                        act.activation(v_hi[i.r % 2], V_BANK, ACT.Copy).then_inc(v_hi_set, 1)
                    if i := stage(4):
                        act.wait_ge(turned_new, i.count())
                        if not isinstance(i.q, int) or i.q > 0:
                            act.wait_ge(h_stored[i.r], i.q * 16)
                        act.activation(h_next[i.r], T_NEW_BANK, ACT.Relu).then_inc(h_next_set, 1)
                sweep(act, G, U, 2, 4, body)

            @block.tensor
            def _(pe):
                def body(stage):
                    if i := stage(0):
                        pe.wait_ge(y_set, i.count())
                        wait(pe, h_set, i.count(1))
                        flip(pe, T_BANK, y[i.r % 2], ident, turned)
                    if i := stage(1):
                        pe.wait_ge(v_lo_set, i.count())
                        by_adjacency(pe, U_BANK, adj_hi, adj_lo, v_hi[i.r % 2], v_lo[i.r % 2]).then_inc(u_sum, 1)
                        wait(pe, x_new_set, i.count(1))
                        by_weight(pe, O_BANK, h_feat[i.r % 2], cheb0[:, 0, :])
                        for row in (bias_hi, bias_lo):
                            pe.matmul(O_BANK, ones_hi[:], row[:], start=False, stop=False, skip_group_check=True)
                    if i := stage(0):
                        pe.wait_ge(h_set, i.count())
                        wait(pe, v_lo_set, i.count(1))
                        by_weight(pe, V_BANK, h_feat[i.r % 2], cheb0[:, 2, :]).then_inc(v_sum, 1)
                    if i := stage(1):
                        pe.wait_ge(u_lo_set, i.count())
                        by_adjacency(pe, O_BANK, adj_hi, adj_lo, u_hi[i.r % 2], u_lo[i.r % 2]).then_inc(o_sum, 1)
                    if i := stage(0):
                        wait(pe, u_lo_set, i.count(1))
                        by_weight(pe, U_BANK, h_feat[i.r % 2], cheb0[:, 1, :])
                    if i := stage(4):
                        pe.wait_ge(y_new_set, i.count())
                        wait(pe, h_next_set, i.count(1))
                        flip(pe, T_NEW_BANK, y_new[i.r % 2], ident, turned_new)
                sweep(pe, G, U, 2, 4, body)


def layer1(nc, psum, sem, h_store, h_stored, ident, adj_hi, adj_lo, gate_hi, gate_lo, gate_b):
    U = 4
    W4, W34, W5, U3, U5 = range(5)
    with ExitStack() as ctx:
        def ring(name, n, dt=F32):
            t = ctx.enter_context(nc.sbuf_tensor("l1_" + name, [P, n, W], dt))
            return [t[:, k] for k in range(n)]

        h, h_new = ring("h", 4), ring("h_new", 4)
        h_hi, h_lo = ring("h_hi", 2, F32R), ring("h_lo", 2, F32R)
        ht_hi, ht_lo = ring("ht_hi", 2, F32R), ring("ht_lo", 2, F32R)
        m_hi, m_lo = ring("m_hi", 2, F32R), ring("m_lo", 2, F32R)
        r_gate, z_gate, rh, cand = ring("r_gate", 2), ring("z_gate", 2), ring("rh", 2), ring("cand", 2)
        rh_hi, rh_lo = ring("rh_hi", 2, F32R), ring("rh_lo", 2, F32R)
        step, zstep = ring("step", 2), ring("zstep", 2)
        h_landed = [sem(f"l1_h_landed{k}") for k in range(U)]
        names = ("turned", "ht_hi_set", "ht_lo_set", "h_hi_set", "h_lo_set", "m_sum", "m_hi_set", "m_lo_set", "r_sum",
                 "r_set", "z_sum", "z_set", "rh_set", "rh_hi_set", "rh_lo_set", "c_sum", "c_set", "step_set",
                 "zstep_set", "h_new_set")
        (turned, ht_hi_set, ht_lo_set, h_hi_set, h_lo_set, m_sum, m_hi_set, m_lo_set, r_sum, r_set, z_sum, z_set,
         rh_set, rh_hi_set, rh_lo_set, c_sum, c_set, step_set, zstep_set, h_new_set) = (sem("l1_" + n) for n in names)
        T_BANK, M_BANK, RZ_BANK, C_BANK = ([psum[:, 2 * k], psum[:, 2 * k + 1]] for k in range(4))

        def stored_before(i):
            return i.q * 16 + 16 * (G // U)

        def group(i):
            return (i.q % (G // U)) * U + i.r

        with nc.Block() as block:
            @block.sync
            def _(sp):
                def body(stage):
                    if i := stage(0):
                        at = place(sp, group(i))
                        wait(sp, h_new_set, i.count(4))
                        sp.wait_ge(h_stored[i.r], i.q * 16 + 16)
                        sp.dma_start(h[i.r], h_store[:, at]).then_inc(h_landed[i.r], 16)
                    if i := stage(4):
                        at = place(sp, group(i))
                        sp.wait_ge(h_new_set, i.count())
                        sp.dma_start(h_store[:, at], h_new[i.r]).then_inc(h_stored[i.r], 16)
                sweep(sp, ITEMS, U, 2, 4, body)
                for k in range(U):
                    sp.wait_ge(h_stored[k], 16 * ((G + ITEMS) // U))

            @block.gpsimd
            def _(pool):
                def body(stage):
                    if i := stage(2):
                        k = i.r % 2
                        pool.wait_ge(step_set, i.count())
                        pool.wait_ge(z_set, i.count())
                        wait(pool, h_new_set, i.count(2))
                        pool.tensor_tensor(zstep[k], z_gate[k], step[k], ALU.mult).then_inc(zstep_set, 1)
                    if i := stage(1):
                        k = i.r % 2
                        pool.wait_ge(c_set, i.count())
                        wait(pool, zstep_set, i.count(2))
                        pool.tensor_tensor(step[k], cand[k], h[i.r], ALU.subtract).then_inc(step_set, 1)
                sweep(pool, ITEMS, U, 1, 2, body)

            @block.vector
            def _(dve):
                def body(stage):
                    if i := stage(0):
                        k = i.r % 2
                        dve.wait_ge(ht_hi_set, i.count())
                        wait(dve, m_sum, i.count(2))
                        dve.tensor_tensor(ht_lo[k], T_BANK[k], ht_hi[k].bitcast(F32), ALU.subtract).then_inc(ht_lo_set, 1)
                        dve.wait_ge(h_hi_set, i.count())
                        wait(dve, r_sum, i.count(2))
                        dve.tensor_tensor(h_lo[k], h[i.r], h_hi[k].bitcast(F32), ALU.subtract).then_inc(h_lo_set, 1)
                    if i := stage(1):
                        k = i.r % 2
                        dve.wait_ge(r_set, i.count())
                        wait(dve, rh_lo_set, i.count(2))
                        dve.tensor_tensor(rh[k], r_gate[k], h[i.r], ALU.mult).then_inc(rh_set, 1)
                    if i := stage(0):
                        k = i.r % 2
                        dve.wait_ge(m_hi_set, i.count())
                        wait(dve, c_sum, i.count(2))
                        dve.tensor_tensor(m_lo[k], M_BANK[k], m_hi[k].bitcast(F32), ALU.subtract).then_inc(m_lo_set, 1)
                    if i := stage(1):
                        k = i.r % 2
                        dve.wait_ge(rh_hi_set, i.count())
                        wait(dve, c_sum, i.count(2))
                        dve.tensor_tensor(rh_lo[k], rh[k], rh_hi[k].bitcast(F32), ALU.subtract).then_inc(rh_lo_set, 1)
                    if i := stage(2):
                        k = i.r % 2
                        dve.wait_ge(zstep_set, i.count())
                        dve.wait_ge(h_stored[i.r], stored_before(i))
                        dve.tensor_tensor(h_new[i.r], h[i.r], zstep[k], ALU.add).then_inc(h_new_set, 1)
                sweep(dve, ITEMS, U, 1, 2, body)

            @block.scalar
            def _(act):
                def body(stage):
                    if i := stage(0):
                        k = i.r % 2
                        act.wait_ge(turned, i.count())
                        wait(act, m_sum, i.count(2))
                        act.activation(ht_hi[k], T_BANK[k], ACT.Copy).then_inc(ht_hi_set, 1)
                    if i := stage(2):
                        k = i.r % 2
                        act.wait_ge(z_sum, i.count())
                        wait(act, zstep_set, i.count(2))
                        act.activation(z_gate[k], RZ_BANK[k], ACT.Sigmoid, bias=gate_b[:, 1:2]).then_inc(z_set, 1)
                    if i := stage(0):
                        k = i.r % 2
                        act.wait_ge(h_landed[i.r], i.dma())
                        wait(act, r_sum, i.count(2))
                        act.activation(h_hi[k], h[i.r], ACT.Copy).then_inc(h_hi_set, 1)
                    if i := stage(1):
                        k = i.r % 2
                        act.wait_ge(r_sum, i.count())
                        wait(act, rh_set, i.count(2))
                        act.activation(r_gate[k], RZ_BANK[k], ACT.Sigmoid, bias=gate_b[:, 0:1]).then_inc(r_set, 1)
                    if i := stage(2):
                        k = i.r % 2
                        act.wait_ge(c_sum, i.count())
                        wait(act, step_set, i.count(2))
                        act.activation(cand[k], C_BANK[k], ACT.Tanh, bias=gate_b[:, 2:3]).then_inc(c_set, 1)
                    if i := stage(0):
                        k = i.r % 2
                        act.wait_ge(m_sum, i.count())
                        wait(act, c_sum, i.count(2))
                        act.activation(m_hi[k], M_BANK[k], ACT.Copy).then_inc(m_hi_set, 1)
                    if i := stage(1):
                        k = i.r % 2
                        act.wait_ge(rh_set, i.count())
                        wait(act, c_sum, i.count(2))
                        act.activation(rh_hi[k], rh[k], ACT.Copy).then_inc(rh_hi_set, 1)
                sweep(act, ITEMS, U, 1, 2, body)

            @block.tensor
            def _(pe):
                def gate(bank, which, v_hi, v_lo, start, stop):
                    w_hi, w_lo = gate_hi[:, which, :], gate_lo[:, which, :]
                    for n, (w, v) in enumerate(((w_hi, v_hi), (w_hi, v_lo), (w_lo, v_hi))):
                        last = pe.matmul(bank, w, v, start=start and n == 0, stop=stop and n == 2, skip_group_check=True)
                    return last

                def body(stage):
                    if i := stage(0):
                        k = i.r % 2
                        pe.wait_ge(h_landed[i.r], i.dma())
                        wait(pe, ht_lo_set, i.count(2))
                        flip_back(pe, T_BANK[k], h[i.r], ident, turned)
                    if i := stage(1):
                        k = i.r % 2
                        pe.wait_ge(h_lo_set, i.count())
                        wait(pe, z_set, i.count(2))
                        gate(RZ_BANK[k], U3, h_hi[k], h_lo[k], True, False)
                    if i := stage(2):
                        k = i.r % 2
                        wait(pe, c_set, i.count(2))
                        gate(C_BANK[k], W5, m_hi[k], m_lo[k], True, False)
                    if i := stage(1):
                        k = i.r % 2
                        pe.wait_ge(m_lo_set, i.count())
                        gate(RZ_BANK[k], W4, m_hi[k], m_lo[k], False, False).then_inc(r_sum, 1)
                    if i := stage(2):
                        k = i.r % 2
                        pe.wait_ge(rh_lo_set, i.count())
                        gate(C_BANK[k], U5, rh_hi[k], rh_lo[k], False, True).then_inc(c_sum, 1)
                    if i := stage(0):
                        k = i.r % 2
                        pe.wait_ge(ht_lo_set, i.count())
                        wait(pe, m_lo_set, i.count(2))
                        for b in range(GB):
                            n = 0
                            for t in range(NT):
                                c = (t * GB + b) * P
                                for v, a in ((ht_hi, adj_hi), (ht_hi, adj_lo), (ht_lo, adj_hi)):
                                    last = pe.matmul(M_BANK[k][:, b * N:(b + 1) * N], v[k][:, c:c + P], a[:, t, :],
                                                     start=(b == 0 and n == 0), stop=False, skip_group_check=True)
                                    n += 1
                        last.then_inc(m_sum, 1)
                    if i := stage(1):
                        k = i.r % 2
                        pe.wait_ge(r_set, i.count())
                        gate(RZ_BANK[k], W34, m_hi[k], m_lo[k], False, True).then_inc(z_sum, 1)
                sweep(pe, ITEMS, U, 1, 2, body)


def layers23(nc, psum, sem, x_store, h_store, out_dram, ident, adj_tr, adj_hi, adj_lo, cheb3, att_col, att_rep,
             consts, ones):
    U = 2
    LAG = 4
    with ExitStack() as ctx:
        def ring(name, shape=(W,), dt=F32, n=2):
            t = ctx.enter_context(nc.sbuf_tensor("l2_" + name, [P, n, *shape], dt))
            return [t[:, k] for k in range(n)]

        x_in, h_in = ring("x_in"), ring("h_in")
        x2, y2, h2 = ring("x2"), ring("y2"), ring("h2")
        f, leaky, weights = ring("f", (NK, N)), ring("leaky", (NK, N)), ring("weights", (NK, N))
        shift, top, shown, nbias, sums, inv = (ring(n, (NK,)) for n in ("shift", "top", "shown", "nbias", "sums", "inv"))
        values, att, sig = ring("values"), ring("att"), ring("sig")
        x3, y3, h3 = ring("x3"), ring("y3"), ring("h3")
        v_hi, v_lo = ring("v_hi", dt=F32R), ring("v_lo", dt=F32R)
        u2_hi, u2_lo = ring("u2_hi", dt=F32R), ring("u2_lo", dt=F32R)
        u1_hi, u1_lo = ring("u1_hi", dt=F32R), ring("u1_lo", dt=F32R)
        result = ring("result")
        stats2, stats_e, stats3 = (ring(n, (NK, 6)) for n in ("stats2", "stats_e", "stats3"))
        work2, work_e, work3 = (ring(n, (4, NK)) for n in ("work2", "work_e", "work3"))
        mean2, rstd2, mean_e, mean3, rstd3 = (ring(n, (NK,)) for n in ("mean2", "rstd2", "mean_e", "mean3", "rstd3"))
        graph = ring("graph", (6, GB))
        n2, ne, n3 = norm_sems(sem, "l2_n2"), norm_sems(sem, "l2_ne"), norm_sems(sem, "l3_n3")
        x_landed = [sem(f"l2_x_landed{k}") for k in range(U)]
        h_landed = [sem(f"l2_h_landed{k}") for k in range(U)]
        out_stored = [sem(f"l3_out_stored{k}") for k in range(U)]
        names = ("back", "x2_set", "y2_set", "turned2", "h2_set", "e_sum", "graph_sum", "graph_eps", "graph_root",
                 "graph_set", "shift_set", "f_set", "leaky_set", "top_set", "shown_set", "nbias_set", "weights_set",
                 "inv_set", "values_set", "att_sum", "att_set", "sig_set", "x3_set", "y3_set", "turned3", "h3_set",
                 "v_sum", "v_hi_set", "v_lo_set", "u2_sum", "u2_hi_set", "u2_lo_set", "u1_sum", "u1_hi_set", "u1_lo_set",
                 "o_sum", "result_set")
        (back, x2_set, y2_set, turned2, h2_set, e_sum, graph_sum, graph_eps, graph_root, graph_set, shift_set, f_set,
         leaky_set, top_set, shown_set, nbias_set, weights_set, inv_set, values_set, att_sum, att_set, sig_set, x3_set,
         y3_set, turned3, h3_set, v_sum, v_hi_set, v_lo_set, u2_sum, u2_hi_set, u2_lo_set, u1_sum, u1_hi_set,
         u1_lo_set, o_sum, result_set) = (sem("l2_" + n) for n in names)
        BACK, TURN2, ROW_I, ROW_J, VU1, U2O, ATT, COL_J = (psum[:, k] for k in range(8))
        TURN3 = ATT

        with nc.Block() as block:
            @block.sync
            def _(sp):
                def body(stage):
                    if i := stage(0):
                        at = place(sp, i.index())
                        wait(sp, x2_set, i.count(2))
                        wait(sp, back, i.count(2))
                        sp.dma_start(x_in[i.r], x_store[:, at]).then_inc(x_landed[i.r], 16)
                        sp.dma_start(h_in[i.r], h_store[:, at]).then_inc(h_landed[i.r], 16)
                    if i := stage(4):
                        at = place(sp, i.index())
                        sp.wait_ge(result_set, i.count())
                        for b in range(GB):
                            sp.dma_start(out_dram[at * GB + b],
                                         result[i.r].rearrange("p (t b f) -> p b t f", t=NT, b=GB)[:, b]).then_inc(out_stored[i.r], 16)
                sweep(sp, G, U, 3, LAG, body)
                for k in range(U):
                    sp.wait_ge(out_stored[k], 16 * GB * (G // U))

            @block.gpsimd
            def _(pool):
                def body(stage):
                    if i := stage(1):
                        k = i.r
                        wait(pool, y2_set, i.count(2))
                        norm_scalars(pool, n2, i, stats2[k], work2[k], mean2[k], rstd2[k], consts)
                    if i := stage(2):
                        k = i.r
                        pool.wait_ge(att_set, i.count())
                        wait(pool, x3_set, i.count(2))
                        pool.tensor_tensor(sig[k], att[k], ones[:], ALU.add).then_inc(sig_set, 1)
                        wait(pool, y3_set, i.count(2))
                        norm_scalars(pool, n3, i, stats3[k], work3[k], mean3[k], rstd3[k], consts)
                    if i := stage(1):
                        k = i.r
                        var = variance(pool, ne, i, stats_e[k], work_e[k], mean_e[k], N, 0.0, consts)
                        mean_g, var_g, rs, root, lift, minus_rs = (graph[k][:, n, :] for n in range(6))
                        pool.wait_ge(ne["var"], i.count())
                        wait(pool, weights_set, i.count(2))
                        pool.tensor_tensor(mean_g, mean_e[k][:, 0:GB], mean_e[k][:, GB:NK], ALU.add).then_inc(graph_sum, 1)
                        pool.tensor_tensor(var_g, var[:, 0:GB], var[:, GB:NK], ALU.add).then_inc(graph_sum, 1)
                        pool.wait_ge(graph_sum, i.count(per=2))
                        pool.tensor_tensor(var_g, var_g, consts[:, EPS, 0:GB], ALU.add).then_inc(graph_eps, 1)
                        pool.wait_ge(graph_eps, i.count())
                        pool.tensor_tensor(rs, var_g, consts[:, MINUS_HALF, 0:GB], ALU.pow).then_inc(graph_root, 1)
                        pool.tensor_tensor(root, var_g, consts[:, HALF, 0:GB], ALU.pow).then_inc(graph_root, 1)
                        pool.wait_ge(graph_root, i.count(per=2))
                        pool.tensor_tensor(lift, root, mean_g, ALU.subtract).then_inc(graph_set, 1)
                        pool.tensor_scalar(minus_rs, rs, -1.0, 0.0, ALU.mult, ALU.add).then_inc(graph_set, 1)
                sweep(pool, G, U, 3, LAG, body)

            @block.vector
            def _(dve):
                def low(i, hi_set, out_free, ago, out, bank, hi, done):
                    dve.wait_ge(hi_set, i.count())
                    wait(dve, out_free, i.count(ago))
                    dve.tensor_tensor(out, bank, hi.bitcast(F32), ALU.subtract).then_inc(done, 1)

                def body(stage):
                    if i := stage(2):
                        k = i.r
                        dve.wait_ge(graph_set, i.count(per=2))
                        dve.wait_ge(e_sum, i.count())
                        wait(dve, f_set, i.count(2))
                        for b in range(GB):
                            last = dve.tensor_scalar(shift[k][:, b * NT:(b + 1) * NT], COL_J[:, b * NT:(b + 1) * NT],
                                                     graph[k][:, 4, b:b + 1], None, ALU.add)
                        last.then_inc(shift_set, 1)
                        dve.wait_ge(shift_set, i.count())
                        wait(dve, leaky_set, i.count(2))
                        wait(dve, top_set, i.count(2))
                        for b in range(GB):
                            for t in range(NT):
                                c = b * NT + t
                                last = dve.scalar_tensor_tensor(f[k][:, c, :], ROW_I[:, b * N:(b + 1) * N], shift[k][:, c:c + 1],
                                                                adj_tr[:, t, :], ALU.add, ALU.mult)
                        last.then_inc(f_set, 1)
                        dve.wait_ge(f_set, i.count())
                        wait(dve, weights_set, i.count(2))
                        dve.scalar_tensor_tensor(leaky[k], f[k], LEAK, f[k], ALU.mult, ALU.max).then_inc(leaky_set, 1)
                    if i := stage(3):
                        low(i, v_hi_set, u2_sum, 2, v_lo[i.r], VU1, v_hi[i.r], v_lo_set)
                    if i := stage(1):
                        k = i.r
                        dve.wait_ge(back, i.count())
                        dve.wait_ge(x_landed[k], i.dma())
                        wait(dve, x3_set, i.count(2))
                        dve.tensor_tensor(x2[k], BACK, x_in[k], ALU.add).then_inc(x2_set, 1)
                        dve.wait_ge(x2_set, i.count())
                        wait(dve, n2["sums"], i.count(2, per=3))
                        norm_stats(dve, n2, stats2[k], x2[k], D)
                    if i := stage(2):
                        k = i.r
                        wait(dve, shown_set, i.count(2))
                        dve.tensor_reduce(top[k], f[k], AX.X, ALU.max).then_inc(top_set, 1)
                        dve.wait_ge(top_set, i.count())
                        wait(dve, nbias_set, i.count(2))
                        dve.scalar_tensor_tensor(shown[k], top[k], LEAK, top[k], ALU.mult, ALU.max).then_inc(shown_set, 1)
                        dve.wait_ge(shown_set, i.count())
                        wait(dve, weights_set, i.count(2))
                        for b in range(GB):
                            last = dve.tensor_scalar(nbias[k][:, b * NT:(b + 1) * NT], shown[k][:, b * NT:(b + 1) * NT],
                                                     graph[k][:, 5, b:b + 1], None, ALU.mult)
                        last.then_inc(nbias_set, 1)
                    if i := stage(3):
                        low(i, u2_hi_set, u1_sum, 2, u2_lo[i.r], U2O, u2_hi[i.r], u2_lo_set)
                    if i := stage(1):
                        k = i.r
                        dve.wait_ge(n2["rstd"], i.count())
                        wait(dve, turned2, i.count(2))
                        wait(dve, values_set, i.count(2))
                        normalise(dve, y2[k], x2[k], mean2[k], rstd2[k], y2_set)
                    if i := stage(2):
                        k = i.r
                        dve.wait_ge(weights_set, i.count())
                        wait(dve, values_set, i.count(2))
                        dve.reciprocal(inv[k], sums[k]).then_inc(inv_set, 1)
                        dve.wait_ge(inv_set, i.count())
                        wait(dve, att_sum, i.count(2))
                        for t in range(NT):
                            for b in range(GB):
                                n, c = t * GB + b, b * NT + t
                                last = dve.tensor_scalar(values[k][:, n * D:(n + 1) * D], y2[k][:, n * D:(n + 1) * D],
                                                         0.0, inv[k][:, c:c + 1], ALU.max, ALU.mult)
                        last.then_inc(values_set, 1)
                    if i := stage(3):
                        low(i, u1_hi_set, o_sum, 2, u1_lo[i.r], VU1, u1_hi[i.r], u1_lo_set)
                    if i := stage(1):
                        k = i.r
                        dve.wait_ge(e_sum, i.count())
                        wait(dve, ne["sums"], i.count(2, per=3))
                        for b in range(GB):
                            dve.bn_stats(stats_e[k][:, b, :], ROW_I[:, b * N:(b + 1) * N])
                        for b in range(GB):
                            last = dve.bn_stats(stats_e[k][:, GB + b, :], ROW_J[:, b * N:(b + 1) * N])
                        last.then_inc(ne["stats"], 1)
                    if i := stage(2):
                        k = i.r
                        dve.wait_ge(sig_set, i.count())
                        wait(dve, y3_set, i.count(2))
                        wait(dve, result_set, i.count(2))
                        dve.scalar_tensor_tensor(x3[k], sig[k], 0.5, x2[k], ALU.mult, ALU.add).then_inc(x3_set, 1)
                        dve.wait_ge(x3_set, i.count())
                        wait(dve, n3["sums"], i.count(2, per=3))
                        norm_stats(dve, n3, stats3[k], x3[k], D)
                        dve.wait_ge(n3["rstd"], i.count())
                        wait(dve, turned3, i.count(2))
                        normalise(dve, y3[k], x3[k], mean3[k], rstd3[k], y3_set)
                    if i := stage(3):
                        dve.wait_ge(o_sum, i.count())
                        if not isinstance(i.q, int) or i.q > 0:
                            dve.wait_ge(out_stored[i.r], i.q * (16 * GB))
                        dve.tensor_tensor(result[i.r], U2O, x3[i.r], ALU.add).then_inc(result_set, 1)
                sweep(dve, G, U, 3, LAG, body)

            @block.scalar
            def _(act):
                def high(i, summed, out_free, ago, out, bank, done):
                    act.wait_ge(summed, i.count())
                    wait(act, out_free, i.count(ago))
                    act.activation(out, bank, ACT.Copy).then_inc(done, 1)

                def body(stage):
                    if i := stage(3):
                        act.wait_ge(turned3, i.count())
                        wait(act, o_sum, i.count(2))
                        act.activation(h3[i.r], TURN3, ACT.Relu).then_inc(h3_set, 1)
                    if i := stage(3):
                        high(i, v_sum, u2_sum, 2, v_hi[i.r], VU1, v_hi_set)
                    if i := stage(2):
                        k = i.r
                        act.wait_ge(leaky_set, i.count())
                        act.wait_ge(nbias_set, i.count())
                        wait(act, att_sum, i.count(2))
                        wait(act, inv_set, i.count(2))
                        for c in range(NK):
                            last = act.activation(weights[k][:, c, :], leaky[k][:, c, :], ACT.Exp, bias=nbias[k][:, c:c + 1],
                                                  scale=graph[k][:, 2, c // NT:c // NT + 1], accum_out=sums[k][:, c:c + 1])
                        last.then_inc(weights_set, 1)
                    if i := stage(3):
                        high(i, u2_sum, u1_sum, 2, u2_hi[i.r], U2O, u2_hi_set)
                    if i := stage(1):
                        act.wait_ge(turned2, i.count())
                        wait(act, e_sum, i.count(2))
                        act.activation(h2[i.r], TURN2, ACT.Relu).then_inc(h2_set, 1)
                    if i := stage(3):
                        high(i, u1_sum, o_sum, 2, u1_hi[i.r], VU1, u1_hi_set)
                    if i := stage(2):
                        act.wait_ge(att_sum, i.count())
                        wait(act, sig_set, i.count(2))
                        act.activation(att[i.r], ATT, ACT.Tanh, scale=0.5).then_inc(att_set, 1)
                sweep(act, G, U, 3, LAG, body)

            @block.tensor
            def _(pe):
                def body(stage):
                    if i := stage(2 + 1):
                        pe.wait_ge(y3_set, i.count())
                        pe.wait_ge(att_set, i.count())
                        flip(pe, TURN3, y3[i.r], ident, turned3)
                    if i := stage(1):
                        pe.wait_ge(h_landed[i.r], i.dma())
                        wait(pe, x2_set, i.count(1))
                        flip_back(pe, BACK, h_in[i.r], ident, back)
                    if i := stage(3):
                        pe.wait_ge(h3_set, i.count())
                        wait(pe, u1_lo_set, i.count(1))
                        by_weight(pe, VU1, h3[i.r], cheb3[:, 3, :]).then_inc(v_sum, 1)
                        wait(pe, result_set, i.count(1))
                        by_weight(pe, U2O, h3[i.r], cheb3[:, 2, :])
                        pe.wait_ge(v_lo_set, i.count())
                        by_adjacency(pe, U2O, adj_hi, adj_lo, v_hi[i.r], v_lo[i.r]).then_inc(u2_sum, 1)
                        by_weight(pe, VU1, h3[i.r], cheb3[:, 1, :])
                    if i := stage(1):
                        pe.wait_ge(y2_set, i.count())
                        wait(pe, h2_set, i.count(1))
                        flip(pe, TURN2, y2[i.r], ident, turned2)
                    if i := stage(3):
                        pe.wait_ge(u2_lo_set, i.count())
                        by_adjacency(pe, VU1, adj_hi, adj_lo, u2_hi[i.r], u2_lo[i.r]).then_inc(u1_sum, 1)
                    if i := stage(2):
                        k = i.r
                        pe.wait_ge(values_set, i.count())
                        wait(pe, h3_set, i.count(1))
                        first = True
                        for t in range(NT):
                            for b in range(GB):
                                n = t * GB + b
                                for j in range(NT):
                                    last = pe.matmul(ATT[:, n * D:(n + 1) * D], weights[k][:, b * NT + j, t * P:(t + 1) * P],
                                                     values[k][:, (j * GB + b) * D:(j * GB + b + 1) * D],
                                                     start=first, stop=False, skip_group_check=True)
                                    first = False
                        last.then_inc(att_sum, 1)
                    if i := stage(1):
                        k = i.r
                        pe.wait_ge(h2_set, i.count())
                        wait(pe, f_set, i.count(1))
                        pe.matmul(ROW_I, att_rep[:, 0, :], h2[k], start=True, stop=True)
                        wait(pe, ne["stats"], i.count(1))
                        pe.matmul(ROW_J, att_rep[:, 1, :], h2[k], start=True, stop=True)
                        wait(pe, shift_set, i.count(1))
                        for c in range(NK):
                            last = pe.matmul(COL_J[:, c:c + 1], h2[k][:, c * P:(c + 1) * P], att_col[:, 1:2],
                                             start=(c == 0), stop=False, skip_group_check=True)
                        last.then_inc(e_sum, 1)
                    if i := stage(3):
                        by_weight(pe, U2O, h3[i.r], cheb3[:, 0, :])
                        pe.wait_ge(u1_lo_set, i.count())
                        by_adjacency(pe, U2O, adj_hi, adj_lo, u1_hi[i.r], u1_lo[i.r]).then_inc(o_sum, 1)
                sweep(pe, G, U, 3, LAG, body)


_INS = ['x', 'adj', 'L0_gnn_Theta1', 'L0_gnn_bias', 'L1_gnn_w3_w', 'L1_gnn_w3_b', 'L1_gnn_u3_w', 'L1_gnn_u3_b',
        'L1_gnn_w4_w', 'L1_gnn_w4_b', 'L1_gnn_w5_w', 'L1_gnn_w5_b', 'L1_gnn_u5_w', 'L1_gnn_u5_b', 'L2_gnn_a',
        'L3_gnn_weight_1']
_OUTS = [((B, N, D), 'float32')]


def kernel(**inputs):
    import numpy as _np
    import concourse.bacc as _bacc
    from concourse import mybir as _mybir
    from concourse.bass_utils import run_bass_kernel_spmd as _run

    nc = _bacc.Bacc("TRN2", target_bir_lowering=False, num_devices=1)
    arrays, args = {}, []
    for name in _INS:
        a = _np.ascontiguousarray(inputs[name])
        arrays[f"in_{name}_dram"] = a
        args.append(nc.dram_tensor(f"in_{name}_dram", a.shape, _mybir.dt.from_np(a.dtype), kind="ExternalInput").ap())
    for i, (shape, dtype) in enumerate(_OUTS):
        dt = _mybir.dt.from_np(_np.dtype(dtype))
        args.append(nc.dram_tensor(f"out_{i}_dram", shape, dt, kind="ExternalOutput").ap())
    build(nc, *args)
    r = _run(nc, [arrays], core_ids=[0])
    return r.results[0]["out_0_dram"]
```

```python
from contextlib import ExitStack

import concourse.bass as bass
from concourse import mybir

F32 = mybir.dt.float32
F32R = mybir.dt.float32r
ALU = mybir.AluOpType
ACT = mybir.ActivationFunctionType
AX = mybir.AxisListType

P = 128
B, N, D = 32, 256, 128
NT = N // P
GB = 2
G = B // GB
NK = NT * GB
W = GB * N
STEPS = 5
ITEMS = STEPS * G
LN_EPS = 1e-5
ATT_EPS = 1e-14
LEAK = 0.2
MINUS_HALF, HALF, QUARTER, EPS = range(4)


class Item:

    def __init__(self, q, r, unroll, items):
        self.q, self.r, self.u, self.items = q, r, unroll, items

    def count(self, ago=0, per=1):
        at = per * (self.r - ago + 1)
        if isinstance(self.q, int):
            return min(per * self.u * self.q + at, per * self.items)
        return self.q * (per * self.u) + at

    def dma(self, per=1):
        return self.q * (16 * per) + 16 * per

    def before(self, ago):
        r = self.r - ago
        q = self.q + r // self.u if r // self.u else self.q
        return None if isinstance(q, int) and q < 0 else Item(q, r % self.u, self.u, self.items)

    def index(self):
        return self.q * self.u + self.r


def place(eng, index):
    return index if isinstance(index, int) else eng.snap(index)


def wait(eng, sem, value):
    if not isinstance(value, int) or value > 0:
        eng.wait_ge(sem, value)


def sweep(eng, items, unroll, head, lag, body):
    def slot(q, j, bounded):
        def stage(behind):
            r = j - behind
            q_, r_ = q + r // unroll if r // unroll else q, r % unroll
            if bounded and not 0 <= unroll * q_ + r_ < items:
                return None
            return Item(q_, r_, unroll, items)
        body(stage)

    for q in range(head):
        for j in range(unroll):
            slot(q, j, True)
    with eng.Fori(head, items // unroll, 1) as q:
        for j in range(unroll):
            slot(q, j, False)
    for s in range(items, items + lag):
        slot(s // unroll, s % unroll, True)


def build(nc, x, adj, Theta1, bias0, w3_w, w3_b, u3_w, u3_b, w4_w, w4_b, w5_w, w5_b, u5_w, u5_b, att, weight_1, out):
    x_dram = x.rearrange("b (t p) f -> b p t f", p=P)
    out_dram = out.rearrange("b (t p) f -> b p t f", p=P)

    with ExitStack() as whole:
        def sb(name, shape, dt=F32, ctx=whole):
            return ctx.enter_context(nc.sbuf_tensor(name, shape, dt))

        def sem(name):
            return whole.enter_context(nc.semaphore(name))

        psum = whole.enter_context(nc.psum_tensor("psum", [P, 8, 512], F32))

        x_store = sb("x_store", [P, G, W])
        h_store = sb("h_store", [P, G, W])

        ident = sb("ident", [P, P])
        adj_nat = sb("adj_nat", [P, NT, N])
        adj_tr = sb("adj_tr", [P, NT, N])
        adj_nat_hi, adj_nat_lo = sb("adj_nat_hi", [P, NT, N], F32R), sb("adj_nat_lo", [P, NT, N], F32R)
        adj_tr_hi, adj_tr_lo = sb("adj_tr_hi", [P, NT, N], F32R), sb("adj_tr_lo", [P, NT, N], F32R)
        cheb0 = sb("cheb0", [P, 3, P])
        cheb3 = sb("cheb3", [P, 4, P])
        gate_w = sb("gate_w", [P, 5, P])
        gate_hi, gate_lo = sb("gate_hi", [P, 5, P], F32R), sb("gate_lo", [P, 5, P], F32R)
        gate_b = sb("gate_b", [P, 3])
        ones_hi = sb("ones_hi", [1, P], F32R)
        bias_row = sb("bias_row", [1, W])
        bias_hi, bias_lo = sb("bias_hi", [1, W], F32R), sb("bias_lo", [1, W], F32R)
        att_col = sb("att_col", [P, 2])
        att_rep = sb("att_rep", [P, 2, P])
        consts = sb("consts", [P, 4, NK])
        ones = sb("ones", [P, W])

        x_in_landed = [sem(f"x_in_landed{r}") for r in range(4)]
        x_stored = [sem(f"x_stored{r}") for r in range(4)]
        h_stored = [sem(f"h_stored{r}") for r in range(4)]

        prepare(nc, psum, sem, sb, ident, adj, adj_nat, adj_tr, adj_nat_hi, adj_nat_lo, adj_tr_hi, adj_tr_lo,
                Theta1, cheb0, weight_1, cheb3, (w3_w, w4_w, w5_w, u3_w, u5_w), gate_w, gate_hi, gate_lo,
                (w3_b, w4_b, w5_b, u3_b, u5_b), gate_b, bias0, ones_hi, bias_row, bias_hi, bias_lo,
                att, att_col, att_rep, consts, ones)
        layer0(nc, psum, sem, x_dram, x_store, h_store, x_in_landed, x_stored, h_stored, ident,
               adj_nat_hi, adj_nat_lo, cheb0, ones_hi, bias_hi, bias_lo, consts)
        layer1(nc, psum, sem, h_store, h_stored, ident, adj_tr_hi, adj_tr_lo, gate_hi, gate_lo, gate_b)
        layers23(nc, psum, sem, x_store, h_store, out_dram, ident, adj_tr, adj_tr_hi, adj_tr_lo, cheb3,
                 att_col, att_rep, consts, ones)


def prepare(nc, psum, sem, sb, ident, adj, adj_nat, adj_tr, adj_nat_hi, adj_nat_lo, adj_tr_hi, adj_tr_lo,
            Theta1, cheb0, weight_1, cheb3, weights, gate_w, gate_hi, gate_lo,
            biases, gate_b, bias0, ones_hi, bias_row, bias_hi, bias_lo, att, att_col, att_rep, consts, ones):
    w3_w, w4_w, w5_w, u3_w, u5_w = weights
    with ExitStack() as ctx:
        theta = sb("theta", [P, 5, P], F32, ctx)
        cheb_raw = sb("cheb_raw", [P, P, 7], F32, ctx)
        gate_raw = sb("gate_raw", [P, 8, P], F32, ctx)
        gate_sum = sb("gate_sum", [P, 5, P], F32, ctx)
        bias_raw = sb("bias_raw", [P, 5], F32, ctx)
        loaded, adj_loaded = sem("loaded"), sem("adj_loaded")
        zeroed, ident_set, consts_set, ones_set = sem("zeroed"), sem("ident_set"), sem("consts_set"), sem("ones_set")
        adj_turned, adj_tr_set, adj_split, adj_hi_set = sem("adj_turned"), sem("adj_tr_set"), sem("adj_split"), sem("adj_hi_set")
        summed, turned, gate_set, gate_hi_set, w34 = sem("summed"), sem("turned"), sem("gate_set"), sem("gate_hi_set"), sem("w34")
        cheb_part, row_hi = sem("cheb_part"), sem("row_hi")
        LOADS = 16 * (7 + 5 + NK + 2)
        with nc.Block() as block:
            @block.sync
            def _(sp):
                sp.dma_start(adj_nat[:], adj.rearrange("(t p) w -> p t w", p=P)).then_inc(adj_loaded, 16)
                sp.dma_start(gate_raw[:, 0:2, :], w4_w.rearrange("o (c i) -> o c i", i=P)).then_inc(loaded, 16)
                sp.dma_start(gate_raw[:, 2:4, :], w3_w.rearrange("o (c i) -> o c i", i=P)).then_inc(loaded, 16)
                sp.dma_start(gate_raw[:, 4:6, :], w5_w.rearrange("o (c i) -> o c i", i=P)).then_inc(loaded, 16)
                sp.dma_start(gate_raw[:, 6, :], u3_w).then_inc(loaded, 16)
                sp.dma_start(gate_raw[:, 7, :], u5_w).then_inc(loaded, 16)
                sp.dma_start(theta[:], Theta1.rearrange("(k f) o -> f k o", f=P)).then_inc(loaded, 16)
                sp.dma_start(cheb_raw[:], weight_1).then_inc(loaded, 16)
                for k, b in enumerate(biases):
                    sp.dma_start(bias_raw[:, k:k + 1], b.rearrange("(p o) -> p o", o=1)).then_inc(loaded, 16)
                for k in range(NK):
                    sp.dma_start(bias_row[:, k * P:(k + 1) * P], bias0.rearrange("(o f) -> o f", o=1)).then_inc(loaded, 16)
                for k in range(2):
                    sp.dma_start(att_col[:, k:k + 1], att[k * D:(k + 1) * D, :]).then_inc(loaded, 16)


            @block.gpsimd
            def _(pool):
                nc.gpsimd.memset(ident[:], 0.0).then_inc(zeroed, 1)
                pool.wait_ge(zeroed, 1)
                nc.gpsimd.affine_select(out=ident[:], in_=ident[:], compare_op=ALU.not_equal, fill=1.0, base=0,
                                        pattern=[[-1, P]], channel_multiplier=1).then_inc(ident_set, 1)
                for which, value in ((MINUS_HALF, -0.5), (HALF, 0.5), (QUARTER, 0.25), (EPS, ATT_EPS)):
                    nc.gpsimd.memset(consts[:, which], value).then_inc(consts_set, 1)

            @block.vector
            def _(dve):
                nc.vector.memset(ones[:], 1.0).then_inc(ones_set, 1)
                dve.wait_ge(adj_loaded, 16)
                dve.wait_ge(adj_hi_set, 1)
                nc.vector.tensor_tensor(adj_nat_lo[:], adj_nat[:], adj_nat_hi[:].bitcast(F32), ALU.subtract).then_inc(adj_split, 1)
                dve.wait_ge(adj_turned, 1)
                nc.vector.tensor_copy(adj_tr[:].rearrange("p t n -> p (t n)"), psum[:, 0, :]).then_inc(adj_tr_set, 1)
                dve.wait_ge(adj_hi_set, 2)
                dve.wait_ge(adj_tr_set, 1)
                nc.vector.tensor_tensor(adj_tr_lo[:], adj_tr[:], adj_tr_hi[:].bitcast(F32), ALU.subtract).then_inc(adj_split, 1)
                dve.wait_ge(loaded, LOADS)
                halves = gate_raw[:, 0:6, :].rearrange("p (k c) i -> p k c i", c=2)
                nc.vector.tensor_tensor(gate_sum[:, 0:3, :], halves[:, :, 0, :], halves[:, :, 1, :], ALU.add).then_inc(summed, 1)
                nc.vector.tensor_copy(gate_sum[:, 3:5, :], gate_raw[:, 6:8, :]).then_inc(summed, 1)
                nc.vector.tensor_tensor(cheb0[:, 1, :], theta[:, 1, :], theta[:, 3, :], ALU.add).then_inc(cheb_part, 1)
                nc.vector.tensor_tensor(cheb0[:, 2, :], theta[:, 2, :], theta[:, 4, :], ALU.add).then_inc(cheb_part, 1)
                dve.wait_ge(cheb_part, 2)
                nc.vector.tensor_tensor(cheb0[:, 0, :], theta[:, 0, :], cheb0[:, 2, :], ALU.subtract).then_inc(cheb_part, 1)
                dve.wait_ge(cheb_part, 3)
                nc.vector.tensor_scalar(cheb0[:, 2, :], cheb0[:, 2, :], 2.0, None, ALU.mult).then_inc(cheb_part, 1)
                nc.vector.tensor_copy(cheb3[:, 0, :], cheb_raw[:, :, 0]).then_inc(cheb_part, 1)
                for k in range(1, 4):
                    nc.vector.tensor_tensor(cheb3[:, k, :], cheb_raw[:, :, k], cheb_raw[:, :, k + 3], ALU.add).then_inc(cheb_part, 1)
                for k, other in ((0, 1), (1, 0), (2, 2)):
                    nc.vector.tensor_tensor(gate_b[:, k:k + 1], bias_raw[:, other:other + 1],
                                            bias_raw[:, 3 + k // 2:4 + k // 2], ALU.add).then_inc(cheb_part, 1)
                for k in range(2):
                    nc.vector.tensor_scalar(att_rep[:, k, :], ones[:, 0:P], att_col[:, k:k + 1], None, ALU.mult).then_inc(cheb_part, 1)
                nc.vector.tensor_copy(ones_hi[:], ones[0:1, 0:P]).then_inc(cheb_part, 1)
                dve.wait_ge(row_hi, 1)
                nc.vector.tensor_tensor(bias_lo[:], bias_row[:], bias_hi[:].bitcast(F32), ALU.subtract).then_inc(cheb_part, 1)
                dve.wait_ge(turned, 1)
                nc.vector.tensor_copy(gate_w[:, 0:4, :].rearrange("p k o -> p (k o)"), psum[:, 1, :]).then_inc(gate_set, 1)
                nc.vector.tensor_copy(gate_w[:, 4, :], psum[:, 2, 0:P]).then_inc(gate_set, 1)
                dve.wait_ge(gate_set, 2)
                nc.vector.tensor_tensor(gate_w[:, 1, :], gate_w[:, 1, :], gate_w[:, 0, :], ALU.subtract).then_inc(w34, 1)
                dve.wait_ge(gate_hi_set, 1)
                nc.vector.tensor_tensor(gate_lo[:], gate_w[:], gate_hi[:].bitcast(F32), ALU.subtract).then_inc(gate_set, 1)

            @block.scalar
            def _(act):
                act.wait_ge(adj_loaded, 16)
                nc.scalar.activation(adj_nat_hi[:], adj_nat[:], ACT.Copy).then_inc(adj_hi_set, 1)
                act.wait_ge(adj_tr_set, 1)
                nc.scalar.activation(adj_tr_hi[:], adj_tr[:], ACT.Copy).then_inc(adj_hi_set, 1)
                act.wait_ge(loaded, LOADS)
                nc.scalar.activation(bias_hi[:], bias_row[:], ACT.Copy).then_inc(row_hi, 1)
                act.wait_ge(w34, 1)
                nc.scalar.activation(gate_hi[:], gate_w[:], ACT.Copy).then_inc(gate_hi_set, 1)

            @block.tensor
            def _(pe):
                pe.wait_ge(ident_set, 1)
                pe.wait_ge(adj_loaded, 16)
                for t in range(NT):
                    for u in range(NT):
                        last = nc.tensor.transpose(psum[:, 0, (u * NT + t) * P:(u * NT + t + 1) * P],
                                                   adj_nat[:, t, u * P:(u + 1) * P], ident[:])
                last.then_inc(adj_turned, 1)
                pe.wait_ge(summed, 2)
                for k in range(5):
                    last = nc.tensor.transpose(psum[:, 1 + k // 4, (k % 4) * P:(k % 4 + 1) * P], gate_sum[:, k, :], ident[:])
                last.then_inc(turned, 1)


def norm_sems(sem, name):
    return {k: sem(f"{name}_{k}") for k in ("stats", "sums", "scaled", "quarter", "var", "rstd")}


def norm_stats(dve, s, stats, tile, width):
    for k in range(NK):
        last = dve.bn_stats(stats[:, k, :], tile[:, k * width:(k + 1) * width])
    last.then_inc(s["stats"], 1)


def variance(pool, s, item, stats, work, mean, count, eps, consts):
    mean_e, m2_e, mean_o, m2_o = (stats[:, :, k] for k in (1, 2, 4, 5))
    total, diff, dev, square = (work[:, k, :] for k in range(4))
    pool.wait_ge(s["stats"], item.count())
    pool.tensor_tensor(total, mean_e, mean_o, ALU.add).then_inc(s["sums"], 1)
    pool.tensor_tensor(diff, mean_e, mean_o, ALU.subtract).then_inc(s["sums"], 1)
    pool.tensor_tensor(dev, m2_e, m2_o, ALU.add).then_inc(s["sums"], 1)
    pool.wait_ge(s["sums"], item.count(per=3))
    pool.tensor_tensor(square, diff, diff, ALU.mult).then_inc(s["scaled"], 1)
    pool.tensor_scalar(mean, total, 0.5, 0.0, ALU.mult, ALU.add).then_inc(s["scaled"], 1)
    pool.tensor_scalar(dev, dev, 1.0 / count, eps, ALU.mult, ALU.add).then_inc(s["scaled"], 1)
    pool.wait_ge(s["scaled"], item.count(per=3))
    pool.tensor_tensor(square, square, consts[:, QUARTER], ALU.mult).then_inc(s["quarter"], 1)
    pool.wait_ge(s["quarter"], item.count())
    pool.tensor_tensor(dev, dev, square, ALU.add).then_inc(s["var"], 1)
    return dev


def norm_scalars(pool, s, item, stats, work, mean, rstd, consts):
    dev = variance(pool, s, item, stats, work, mean, D, LN_EPS, consts)
    pool.wait_ge(s["var"], item.count())
    pool.tensor_tensor(rstd, dev, consts[:, MINUS_HALF], ALU.pow).then_inc(s["rstd"], 1)


def normalise(dve, tile, source, mean, rstd, done):
    for k in range(NK):
        last = dve.tensor_scalar(tile[:, k * D:(k + 1) * D], source[:, k * D:(k + 1) * D],
                                 mean[:, k:k + 1], rstd[:, k:k + 1], ALU.subtract, ALU.mult)
    last.then_inc(done, 1)


def flip(pe, bank, tile, ident, done):
    for t in range(NT):
        for b in range(GB):
            k, c = t * GB + b, b * NT + t
            last = pe.transpose(bank[:, c * P:(c + 1) * P], tile[:, k * P:(k + 1) * P], ident[:])
    last.then_inc(done, 1)


def flip_back(pe, bank, tile, ident, done):
    for t in range(NT):
        for b in range(GB):
            k, c = t * GB + b, b * NT + t
            last = pe.transpose(bank[:, k * P:(k + 1) * P], tile[:, c * P:(c + 1) * P], ident[:])
    last.then_inc(done, 1)


def by_weight(pe, bank, h_feat, weight):
    for t in range(NT):
        for b in range(GB):
            k, c = t * GB + b, b * NT + t
            last = pe.matmul(bank[:, k * P:(k + 1) * P], h_feat[:, c * P:(c + 1) * P], weight,
                             start=(k == 0), stop=False, skip_group_check=True)
    return last


def by_adjacency(pe, bank, mat_hi, mat_lo, v_hi, v_lo):
    for n in range(NT):
        for m in range(NT):
            for left, right in ((mat_hi, v_hi), (mat_hi, v_lo), (mat_lo, v_hi)):
                last = pe.matmul(bank[:, n * GB * D:(n + 1) * GB * D], left[:, m, n * P:(n + 1) * P],
                                 right[:, m * GB * D:(m + 1) * GB * D], start=False, stop=False, skip_group_check=True)
    return last


def layer0(nc, psum, sem, x_dram, x_store, h_store, x_in_landed, x_stored, h_stored, ident,
           adj_hi, adj_lo, cheb0, ones_hi, bias_hi, bias_lo, consts):
    U = 4
    with ExitStack() as ctx:
        def ring(name, n, shape=(W,), dt=F32):
            t = ctx.enter_context(nc.sbuf_tensor("l0_" + name, [P, n, *shape], dt))
            return [t[:, k] for k in range(n)]

        x_in, x_new = ring("x_in", 4), ring("x_new", 4)
        y, y_new = ring("y", 2), ring("y_new", 2)
        h_feat, h_next = ring("h_feat", 2), ring("h_next", 4)
        v_hi, v_lo = ring("v_hi", 2, dt=F32R), ring("v_lo", 2, dt=F32R)
        u_hi, u_lo = ring("u_hi", 2, dt=F32R), ring("u_lo", 2, dt=F32R)
        stats, stats_new = ring("stats", 2, (NK, 6)), ring("stats_new", 2, (NK, 6))
        work, work_new = ring("work", 2, (4, NK)), ring("work_new", 2, (4, NK))
        mean, rstd = ring("mean", 2, (NK,)), ring("rstd", 2, (NK,))
        mean_new, rstd_new = ring("mean_new", 2, (NK,)), ring("rstd_new", 2, (NK,))
        n_in, n_out = norm_sems(sem, "l0_in"), norm_sems(sem, "l0_out")
        y_set, y_new_set = sem("l0_y_set"), sem("l0_y_new_set")
        turned, turned_new = sem("l0_turned"), sem("l0_turned_new")
        h_set, h_next_set = sem("l0_h_set"), sem("l0_h_next_set")
        v_sum, v_hi_set, v_lo_set = sem("l0_v_sum"), sem("l0_v_hi_set"), sem("l0_v_lo_set")
        u_sum, u_hi_set, u_lo_set = sem("l0_u_sum"), sem("l0_u_hi_set"), sem("l0_u_lo_set")
        o_sum, x_new_set = sem("l0_o_sum"), sem("l0_x_new_set")
        T_BANK, T_NEW_BANK, V_BANK, U_BANK, O_BANK = (psum[:, k] for k in (0, 1, 2, 3, 4))

        with nc.Block() as block:
            @block.sync
            def _(sp):
                def body(stage):
                    if i := stage(0):
                        at = place(sp, i.index())
                        wait(sp, x_new_set, i.count(4))
                        for b in range(GB):
                            sp.dma_start(x_in[i.r].rearrange("p (t b f) -> p b t f", t=NT, b=GB)[:, b],
                                         x_dram[at * GB + b]).then_inc(x_in_landed[i.r], 16)
                    if i := stage(7):
                        at = place(sp, i.index())
                        sp.wait_ge(x_new_set, i.count())
                        sp.wait_ge(h_next_set, i.count())
                        sp.dma_start(x_store[:, at], x_new[i.r]).then_inc(x_stored[i.r], 16)
                        sp.dma_start(h_store[:, at], h_next[i.r]).then_inc(h_stored[i.r], 16)
                sweep(sp, G, U, 2, 7, body)
                for k in range(U):
                    sp.wait_ge(x_stored[k], 16 * (G // U))
                for k in range(U):
                    sp.wait_ge(h_stored[k], 16 * (G // U))

            @block.gpsimd
            def _(pool):
                def body(stage):
                    if i := stage(0):
                        wait(pool, y_set, i.count(2))
                        norm_scalars(pool, n_in, i, stats[i.r % 2], work[i.r % 2], mean[i.r % 2], rstd[i.r % 2], consts)
                    if i := stage(3):
                        wait(pool, y_new_set, i.count(2))
                        norm_scalars(pool, n_out, i, stats_new[i.r % 2], work_new[i.r % 2], mean_new[i.r % 2],
                                     rstd_new[i.r % 2], consts)
                sweep(pool, G, U, 2, 3, body)

            @block.vector
            def _(dve):
                def body(stage):
                    if i := stage(0):
                        dve.wait_ge(x_in_landed[i.r], i.dma(per=GB))
                        wait(dve, n_in["sums"], i.count(2, per=3))
                        norm_stats(dve, n_in, stats[i.r % 2], x_in[i.r], D)
                    if i := stage(1):
                        dve.wait_ge(n_in["rstd"], i.count())
                        wait(dve, turned, i.count(2))
                        normalise(dve, y[i.r % 2], x_in[i.r], mean[i.r % 2], rstd[i.r % 2], y_set)
                    if i := stage(2):
                        dve.wait_ge(v_hi_set, i.count())
                        wait(dve, u_sum, i.count(2))
                        dve.tensor_tensor(v_lo[i.r % 2], V_BANK, v_hi[i.r % 2].bitcast(F32), ALU.subtract).then_inc(v_lo_set, 1)
                    if i := stage(3):
                        dve.wait_ge(o_sum, i.count())
                        if not isinstance(i.q, int) or i.q > 0:
                            dve.wait_ge(x_stored[i.r], i.q * 16)
                        dve.scalar_tensor_tensor(x_new[i.r], O_BANK, 0.0, x_in[i.r], ALU.max, ALU.add).then_inc(x_new_set, 1)
                        dve.wait_ge(x_new_set, i.count())
                        wait(dve, n_out["sums"], i.count(2, per=3))
                        norm_stats(dve, n_out, stats_new[i.r % 2], x_new[i.r], D)
                    if i := stage(4):
                        dve.wait_ge(n_out["rstd"], i.count())
                        wait(dve, turned_new, i.count(2))
                        normalise(dve, y_new[i.r % 2], x_new[i.r], mean_new[i.r % 2], rstd_new[i.r % 2], y_new_set)
                    if i := stage(2):
                        dve.wait_ge(u_hi_set, i.count())
                        wait(dve, o_sum, i.count(2))
                        dve.tensor_tensor(u_lo[i.r % 2], U_BANK, u_hi[i.r % 2].bitcast(F32), ALU.subtract).then_inc(u_lo_set, 1)
                sweep(dve, G, U, 2, 4, body)

            @block.scalar
            def _(act):
                def body(stage):
                    if i := stage(0):
                        act.wait_ge(turned, i.count())
                        wait(act, o_sum, i.count(2))
                        act.activation(h_feat[i.r % 2], T_BANK, ACT.Relu).then_inc(h_set, 1)
                    if i := stage(1):
                        act.wait_ge(u_sum, i.count())
                        wait(act, o_sum, i.count(2))
                        act.activation(u_hi[i.r % 2], U_BANK, ACT.Copy).then_inc(u_hi_set, 1)
                    if i := stage(0):
                        act.wait_ge(v_sum, i.count())
                        wait(act, u_sum, i.count(2))
                        act.activation(v_hi[i.r % 2], V_BANK, ACT.Copy).then_inc(v_hi_set, 1)
                    if i := stage(4):
                        act.wait_ge(turned_new, i.count())
                        if not isinstance(i.q, int) or i.q > 0:
                            act.wait_ge(h_stored[i.r], i.q * 16)
                        act.activation(h_next[i.r], T_NEW_BANK, ACT.Relu).then_inc(h_next_set, 1)
                sweep(act, G, U, 2, 4, body)

            @block.tensor
            def _(pe):
                def body(stage):
                    if i := stage(0):
                        pe.wait_ge(y_set, i.count())
                        wait(pe, h_set, i.count(1))
                        flip(pe, T_BANK, y[i.r % 2], ident, turned)
                    if i := stage(1):
                        pe.wait_ge(v_lo_set, i.count())
                        by_adjacency(pe, U_BANK, adj_hi, adj_lo, v_hi[i.r % 2], v_lo[i.r % 2]).then_inc(u_sum, 1)
                        wait(pe, x_new_set, i.count(1))
                        by_weight(pe, O_BANK, h_feat[i.r % 2], cheb0[:, 0, :])
                        for row in (bias_hi, bias_lo):
                            pe.matmul(O_BANK, ones_hi[:], row[:], start=False, stop=False, skip_group_check=True)
                    if i := stage(0):
                        pe.wait_ge(h_set, i.count())
                        wait(pe, v_lo_set, i.count(1))
                        by_weight(pe, V_BANK, h_feat[i.r % 2], cheb0[:, 2, :]).then_inc(v_sum, 1)
                    if i := stage(1):
                        pe.wait_ge(u_lo_set, i.count())
                        by_adjacency(pe, O_BANK, adj_hi, adj_lo, u_hi[i.r % 2], u_lo[i.r % 2]).then_inc(o_sum, 1)
                    if i := stage(0):
                        wait(pe, u_lo_set, i.count(1))
                        by_weight(pe, U_BANK, h_feat[i.r % 2], cheb0[:, 1, :])
                    if i := stage(4):
                        pe.wait_ge(y_new_set, i.count())
                        wait(pe, h_next_set, i.count(1))
                        flip(pe, T_NEW_BANK, y_new[i.r % 2], ident, turned_new)
                sweep(pe, G, U, 2, 4, body)


def layer1(nc, psum, sem, h_store, h_stored, ident, adj_hi, adj_lo, gate_hi, gate_lo, gate_b):
    U = 4
    W4, W34, W5, U3, U5 = range(5)
    with ExitStack() as ctx:
        def ring(name, n, dt=F32):
            t = ctx.enter_context(nc.sbuf_tensor("l1_" + name, [P, n, W], dt))
            return [t[:, k] for k in range(n)]

        h, h_new = ring("h", 4), ring("h_new", 4)
        h_hi, h_lo = ring("h_hi", 2, F32R), ring("h_lo", 2, F32R)
        ht_hi, ht_lo = ring("ht_hi", 2, F32R), ring("ht_lo", 2, F32R)
        m_hi, m_lo = ring("m_hi", 2, F32R), ring("m_lo", 2, F32R)
        r_gate, z_gate, rh, cand = ring("r_gate", 2), ring("z_gate", 2), ring("rh", 2), ring("cand", 2)
        rh_hi, rh_lo = ring("rh_hi", 2, F32R), ring("rh_lo", 2, F32R)
        step, zstep = ring("step", 2), ring("zstep", 2)
        h_landed = [sem(f"l1_h_landed{k}") for k in range(U)]
        names = ("turned", "ht_hi_set", "ht_lo_set", "h_hi_set", "h_lo_set", "m_sum", "m_hi_set", "m_lo_set", "r_sum",
                 "r_set", "z_sum", "z_set", "rh_set", "rh_hi_set", "rh_lo_set", "c_sum", "c_set", "step_set",
                 "zstep_set", "h_new_set")
        (turned, ht_hi_set, ht_lo_set, h_hi_set, h_lo_set, m_sum, m_hi_set, m_lo_set, r_sum, r_set, z_sum, z_set,
         rh_set, rh_hi_set, rh_lo_set, c_sum, c_set, step_set, zstep_set, h_new_set) = (sem("l1_" + n) for n in names)
        T_BANK, M_BANK, RZ_BANK, C_BANK = ([psum[:, 2 * k], psum[:, 2 * k + 1]] for k in range(4))

        def stored_before(i):
            return i.q * 16 + 16 * (G // U)

        def group(i):
            return (i.q % (G // U)) * U + i.r

        with nc.Block() as block:
            @block.sync
            def _(sp):
                def body(stage):
                    if i := stage(0):
                        at = place(sp, group(i))
                        wait(sp, h_new_set, i.count(4))
                        sp.wait_ge(h_stored[i.r], i.q * 16 + 16)
                        sp.dma_start(h[i.r], h_store[:, at]).then_inc(h_landed[i.r], 16)
                    if i := stage(4):
                        at = place(sp, group(i))
                        sp.wait_ge(h_new_set, i.count())
                        sp.dma_start(h_store[:, at], h_new[i.r]).then_inc(h_stored[i.r], 16)
                sweep(sp, ITEMS, U, 2, 4, body)
                for k in range(U):
                    sp.wait_ge(h_stored[k], 16 * ((G + ITEMS) // U))

            @block.gpsimd
            def _(pool):
                def body(stage):
                    if i := stage(2):
                        k = i.r % 2
                        pool.wait_ge(step_set, i.count())
                        pool.wait_ge(z_set, i.count())
                        wait(pool, h_new_set, i.count(2))
                        pool.tensor_tensor(zstep[k], z_gate[k], step[k], ALU.mult).then_inc(zstep_set, 1)
                    if i := stage(1):
                        k = i.r % 2
                        pool.wait_ge(c_set, i.count())
                        wait(pool, zstep_set, i.count(2))
                        pool.tensor_tensor(step[k], cand[k], h[i.r], ALU.subtract).then_inc(step_set, 1)
                sweep(pool, ITEMS, U, 1, 2, body)

            @block.vector
            def _(dve):
                def body(stage):
                    if i := stage(0):
                        k = i.r % 2
                        dve.wait_ge(ht_hi_set, i.count())
                        wait(dve, m_sum, i.count(2))
                        dve.tensor_tensor(ht_lo[k], T_BANK[k], ht_hi[k].bitcast(F32), ALU.subtract).then_inc(ht_lo_set, 1)
                        dve.wait_ge(h_hi_set, i.count())
                        wait(dve, r_sum, i.count(2))
                        dve.tensor_tensor(h_lo[k], h[i.r], h_hi[k].bitcast(F32), ALU.subtract).then_inc(h_lo_set, 1)
                    if i := stage(1):
                        k = i.r % 2
                        dve.wait_ge(r_set, i.count())
                        wait(dve, rh_lo_set, i.count(2))
                        dve.tensor_tensor(rh[k], r_gate[k], h[i.r], ALU.mult).then_inc(rh_set, 1)
                    if i := stage(0):
                        k = i.r % 2
                        dve.wait_ge(m_hi_set, i.count())
                        wait(dve, c_sum, i.count(2))
                        dve.tensor_tensor(m_lo[k], M_BANK[k], m_hi[k].bitcast(F32), ALU.subtract).then_inc(m_lo_set, 1)
                    if i := stage(1):
                        k = i.r % 2
                        dve.wait_ge(rh_hi_set, i.count())
                        wait(dve, c_sum, i.count(2))
                        dve.tensor_tensor(rh_lo[k], rh[k], rh_hi[k].bitcast(F32), ALU.subtract).then_inc(rh_lo_set, 1)
                    if i := stage(2):
                        k = i.r % 2
                        dve.wait_ge(zstep_set, i.count())
                        dve.wait_ge(h_stored[i.r], stored_before(i))
                        dve.tensor_tensor(h_new[i.r], h[i.r], zstep[k], ALU.add).then_inc(h_new_set, 1)
                sweep(dve, ITEMS, U, 1, 2, body)

            @block.scalar
            def _(act):
                def body(stage):
                    if i := stage(0):
                        k = i.r % 2
                        act.wait_ge(turned, i.count())
                        wait(act, m_sum, i.count(2))
                        act.activation(ht_hi[k], T_BANK[k], ACT.Copy).then_inc(ht_hi_set, 1)
                    if i := stage(2):
                        k = i.r % 2
                        act.wait_ge(z_sum, i.count())
                        wait(act, zstep_set, i.count(2))
                        act.activation(z_gate[k], RZ_BANK[k], ACT.Sigmoid, bias=gate_b[:, 1:2]).then_inc(z_set, 1)
                    if i := stage(0):
                        k = i.r % 2
                        act.wait_ge(h_landed[i.r], i.dma())
                        wait(act, r_sum, i.count(2))
                        act.activation(h_hi[k], h[i.r], ACT.Copy).then_inc(h_hi_set, 1)
                    if i := stage(1):
                        k = i.r % 2
                        act.wait_ge(r_sum, i.count())
                        wait(act, rh_set, i.count(2))
                        act.activation(r_gate[k], RZ_BANK[k], ACT.Sigmoid, bias=gate_b[:, 0:1]).then_inc(r_set, 1)
                    if i := stage(2):
                        k = i.r % 2
                        act.wait_ge(c_sum, i.count())
                        wait(act, step_set, i.count(2))
                        act.activation(cand[k], C_BANK[k], ACT.Tanh, bias=gate_b[:, 2:3]).then_inc(c_set, 1)
                    if i := stage(0):
                        k = i.r % 2
                        act.wait_ge(m_sum, i.count())
                        wait(act, c_sum, i.count(2))
                        act.activation(m_hi[k], M_BANK[k], ACT.Copy).then_inc(m_hi_set, 1)
                    if i := stage(1):
                        k = i.r % 2
                        act.wait_ge(rh_set, i.count())
                        wait(act, c_sum, i.count(2))
                        act.activation(rh_hi[k], rh[k], ACT.Copy).then_inc(rh_hi_set, 1)
                sweep(act, ITEMS, U, 1, 2, body)

            @block.tensor
            def _(pe):
                def gate(bank, which, v_hi, v_lo, start, stop):
                    w_hi, w_lo = gate_hi[:, which, :], gate_lo[:, which, :]
                    for n, (w, v) in enumerate(((w_hi, v_hi), (w_hi, v_lo), (w_lo, v_hi))):
                        last = pe.matmul(bank, w, v, start=start and n == 0, stop=stop and n == 2, skip_group_check=True)
                    return last

                def body(stage):
                    if i := stage(0):
                        k = i.r % 2
                        pe.wait_ge(h_landed[i.r], i.dma())
                        wait(pe, ht_lo_set, i.count(2))
                        flip_back(pe, T_BANK[k], h[i.r], ident, turned)
                    if i := stage(1):
                        k = i.r % 2
                        pe.wait_ge(h_lo_set, i.count())
                        wait(pe, z_set, i.count(2))
                        gate(RZ_BANK[k], U3, h_hi[k], h_lo[k], True, False)
                    if i := stage(2):
                        k = i.r % 2
                        wait(pe, c_set, i.count(2))
                        gate(C_BANK[k], W5, m_hi[k], m_lo[k], True, False)
                    if i := stage(1):
                        k = i.r % 2
                        pe.wait_ge(m_lo_set, i.count())
                        gate(RZ_BANK[k], W4, m_hi[k], m_lo[k], False, False).then_inc(r_sum, 1)
                    if i := stage(2):
                        k = i.r % 2
                        pe.wait_ge(rh_lo_set, i.count())
                        gate(C_BANK[k], U5, rh_hi[k], rh_lo[k], False, True).then_inc(c_sum, 1)
                    if i := stage(0):
                        k = i.r % 2
                        pe.wait_ge(ht_lo_set, i.count())
                        wait(pe, m_lo_set, i.count(2))
                        for b in range(GB):
                            n = 0
                            for t in range(NT):
                                c = (t * GB + b) * P
                                for v, a in ((ht_hi, adj_hi), (ht_hi, adj_lo), (ht_lo, adj_hi)):
                                    last = pe.matmul(M_BANK[k][:, b * N:(b + 1) * N], v[k][:, c:c + P], a[:, t, :],
                                                     start=(b == 0 and n == 0), stop=False, skip_group_check=True)
                                    n += 1
                        last.then_inc(m_sum, 1)
                    if i := stage(1):
                        k = i.r % 2
                        pe.wait_ge(r_set, i.count())
                        gate(RZ_BANK[k], W34, m_hi[k], m_lo[k], False, True).then_inc(z_sum, 1)
                sweep(pe, ITEMS, U, 1, 2, body)


def layers23(nc, psum, sem, x_store, h_store, out_dram, ident, adj_tr, adj_hi, adj_lo, cheb3, att_col, att_rep,
             consts, ones):
    U = 4
    with ExitStack() as ctx:
        def ring(name, n, shape=(W,), dt=F32):
            t = ctx.enter_context(nc.sbuf_tensor("l2_" + name, [P, n, *shape], dt))
            return [t[:, k % n] for k in range(U)]

        x_in, h_in = ring("x_in", 2), ring("h_in", 2)
        x2, y2, h2 = ring("x2", 4), ring("y2", 4), ring("h2", 4)
        scores = ring("scores", 2, (NK, N))
        att = ring("att", 2)
        shift, top, nbias, sums, inv = (ring(n, 2, (NK,)) for n in ("shift", "top", "nbias", "sums", "inv"))
        values = ring("values", 2)
        x3, y3, h3 = ring("x3", 2), ring("y3", 2), ring("h3", 2)
        v_hi, v_lo = ring("v_hi", 2, dt=F32R), ring("v_lo", 2, dt=F32R)
        u2_hi, u2_lo = ring("u2_hi", 2, dt=F32R), ring("u2_lo", 2, dt=F32R)
        u1_hi, u1_lo = ring("u1_hi", 2, dt=F32R), ring("u1_lo", 2, dt=F32R)
        result = ring("result", 2)
        stats2, stats_e, stats3 = (ring(n, 4, (NK, 6)) for n in ("stats2", "stats_e", "stats3"))
        work2, work_e, work3 = (ring(n, 4, (4, NK)) for n in ("work2", "work_e", "work3"))
        mean2, rstd2, mean_e, mean3, rstd3 = (ring(n, 4, (NK,)) for n in ("mean2", "rstd2", "mean_e", "mean3", "rstd3"))
        graph = ring("graph", 4, (6, GB))
        n2, ne, n3 = norm_sems(sem, "l2_n2"), norm_sems(sem, "l2_ne"), norm_sems(sem, "l3_n3")
        x_landed = [sem(f"l2_x_landed{k}") for k in range(U)]
        h_landed = [sem(f"l2_h_landed{k}") for k in range(U)]
        out_stored = [sem(f"l3_out_stored{k}") for k in range(U)]
        names = ("back", "x2_set", "y2_set", "turned2", "h2_set", "row_sum", "col_sum", "graph_sum", "graph_eps",
                 "graph_root", "graph_set", "shift_set", "f_set", "leaky_set", "top_set", "nbias_set", "weights_set",
                 "inv_set", "values_set", "att_sum", "att_set", "sig_set", "x3_set", "y3_set", "turned3", "h3_set",
                 "v_sum", "v_hi_set", "v_lo_set", "u2_sum", "u2_hi_set", "u2_lo_set", "u1_sum", "u1_hi_set", "u1_lo_set",
                 "o_sum", "result_set")
        (back, x2_set, y2_set, turned2, h2_set, row_sum, col_sum, graph_sum, graph_eps, graph_root, graph_set, shift_set,
         f_set, leaky_set, top_set, nbias_set, weights_set, inv_set, values_set, att_sum, att_set, sig_set, x3_set,
         y3_set, turned3, h3_set, v_sum, v_hi_set, v_lo_set, u2_sum, u2_hi_set, u2_lo_set, u1_sum, u1_hi_set,
         u1_lo_set, o_sum, result_set) = (sem("l2_" + n) for n in names)
        ATT, TURN2, O_BANK, BACK, ROW_J, TURN3, V_BANK, ROW_I = (psum[:, k] for k in range(8))
        U1_BANK, COL_J, U2_BANK = TURN2, ROW_J, TURN3

        with nc.Block() as block:
            @block.sync
            def _(sp):
                def body(stage):
                    if i := stage(0):
                        at = place(sp, i.index())
                        wait(sp, x2_set, i.count(2))
                        wait(sp, back, i.count(2))
                        sp.dma_start(x_in[i.r], x_store[:, at]).then_inc(x_landed[i.r], 16)
                        sp.dma_start(h_in[i.r], h_store[:, at]).then_inc(h_landed[i.r], 16)
                    if i := stage(7):
                        at = place(sp, i.index())
                        sp.wait_ge(result_set, i.count())
                        for b in range(GB):
                            sp.dma_start(out_dram[at * GB + b],
                                         result[i.r].rearrange("p (t b f) -> p b t f", t=NT, b=GB)[:, b]).then_inc(out_stored[i.r], 16)
                sweep(sp, G, U, 2, 7, body)
                for k in range(U):
                    sp.wait_ge(out_stored[k], 16 * GB * (G // U))

            @block.gpsimd
            def _(pool):
                def body(stage):
                    if i := stage(0):
                        k = i.r
                        wait(pool, y2_set, i.count(4))
                        norm_scalars(pool, n2, i, stats2[k], work2[k], mean2[k], rstd2[k], consts)
                    if i := stage(3):
                        k = i.r
                        wait(pool, y3_set, i.count(4))
                        norm_scalars(pool, n3, i, stats3[k], work3[k], mean3[k], rstd3[k], consts)
                    if i := stage(1):
                        k = i.r
                        var = variance(pool, ne, i, stats_e[k], work_e[k], mean_e[k], N, 0.0, consts)
                        mean_g, var_g, rs, root, lift, minus_rs = (graph[k][:, n, :] for n in range(6))
                        pool.wait_ge(ne["var"], i.count())
                        wait(pool, weights_set, i.count(4))
                        pool.tensor_tensor(mean_g, mean_e[k][:, 0:GB], mean_e[k][:, GB:NK], ALU.add).then_inc(graph_sum, 1)
                        pool.tensor_tensor(var_g, var[:, 0:GB], var[:, GB:NK], ALU.add).then_inc(graph_sum, 1)
                        pool.wait_ge(graph_sum, i.count(per=2))
                        pool.tensor_tensor(var_g, var_g, consts[:, EPS, 0:GB], ALU.add).then_inc(graph_eps, 1)
                        pool.wait_ge(graph_eps, i.count())
                        pool.tensor_tensor(rs, var_g, consts[:, MINUS_HALF, 0:GB], ALU.pow).then_inc(graph_root, 1)
                        pool.tensor_tensor(root, var_g, consts[:, HALF, 0:GB], ALU.pow).then_inc(graph_root, 1)
                        pool.wait_ge(graph_root, i.count(per=2))
                        pool.tensor_tensor(lift, root, mean_g, ALU.subtract).then_inc(graph_set, 1)
                        pool.tensor_scalar(minus_rs, rs, -1.0, 0.0, ALU.mult, ALU.add).then_inc(graph_set, 1)
                    if i := stage(2):
                        pool.wait_ge(att_set, i.count())
                        pool.tensor_tensor(att[i.r], att[i.r], ones[:], ALU.add).then_inc(sig_set, 1)
                sweep(pool, G, U, 2, 3, body)

            @block.vector
            def _(dve):
                def low(i, hi_set, out_free, out, bank, hi, done):
                    dve.wait_ge(hi_set, i.count())
                    wait(dve, out_free, i.count(2))
                    dve.tensor_tensor(out, bank, hi.bitcast(F32), ALU.subtract).then_inc(done, 1)

                def body(stage):
                    if i := stage(0):
                        k = i.r
                        dve.wait_ge(back, i.count())
                        dve.wait_ge(x_landed[k], i.dma())
                        wait(dve, x3_set, i.count(4))
                        dve.tensor_tensor(x2[k], BACK, x_in[k], ALU.add).then_inc(x2_set, 1)
                        dve.wait_ge(x2_set, i.count())
                        wait(dve, n2["sums"], i.count(4, per=3))
                        norm_stats(dve, n2, stats2[k], x2[k], D)
                    if i := stage(5):
                        dve.wait_ge(o_sum, i.count())
                        if before := i.before(2):
                            dve.wait_ge(out_stored[before.r], before.dma(GB))
                        dve.tensor_tensor(result[i.r], O_BANK, x3[i.r], ALU.add).then_inc(result_set, 1)
                    if i := stage(2):
                        k = i.r
                        dve.wait_ge(graph_set, i.count(per=2))
                        dve.wait_ge(col_sum, i.count())
                        wait(dve, f_set, i.count(2))
                        for b in range(GB):
                            last = dve.tensor_scalar(shift[k][:, b * NT:(b + 1) * NT], COL_J[:, b * NT:(b + 1) * NT],
                                                     graph[k][:, 4, b:b + 1], None, ALU.add)
                        last.then_inc(shift_set, 1)
                        dve.wait_ge(shift_set, i.count())
                        wait(dve, att_sum, i.count(2))
                        for b in range(GB):
                            for t in range(NT):
                                c = b * NT + t
                                last = dve.scalar_tensor_tensor(scores[k][:, c, :], ROW_I[:, b * N:(b + 1) * N],
                                                                shift[k][:, c:c + 1], adj_tr[:, t, :], ALU.add, ALU.mult)
                        last.then_inc(f_set, 1)
                        dve.wait_ge(f_set, i.count())
                        dve.scalar_tensor_tensor(scores[k], scores[k], LEAK, scores[k], ALU.mult, ALU.max).then_inc(leaky_set, 1)
                    if i := stage(4):
                        low(i, v_hi_set, u2_sum, v_lo[i.r], V_BANK, v_hi[i.r], v_lo_set)
                    if i := stage(3):
                        k = i.r
                        dve.wait_ge(sig_set, i.count())
                        wait(dve, y3_set, i.count(2))
                        wait(dve, result_set, i.count(2))
                        dve.scalar_tensor_tensor(x3[k], att[k], 0.5, x2[k], ALU.mult, ALU.add).then_inc(x3_set, 1)
                        dve.wait_ge(x3_set, i.count())
                        wait(dve, n3["sums"], i.count(4, per=3))
                        norm_stats(dve, n3, stats3[k], x3[k], D)
                    if i := stage(2):
                        k = i.r
                        dve.wait_ge(leaky_set, i.count())
                        wait(dve, nbias_set, i.count(2))
                        dve.tensor_reduce(top[k], scores[k], AX.X, ALU.max).then_inc(top_set, 1)
                        dve.wait_ge(top_set, i.count())
                        wait(dve, weights_set, i.count(2))
                        for b in range(GB):
                            last = dve.tensor_scalar(nbias[k][:, b * NT:(b + 1) * NT], top[k][:, b * NT:(b + 1) * NT],
                                                     graph[k][:, 5, b:b + 1], None, ALU.mult)
                        last.then_inc(nbias_set, 1)
                    if i := stage(4):
                        low(i, u2_hi_set, u1_sum, u2_lo[i.r], U2_BANK, u2_hi[i.r], u2_lo_set)
                    if i := stage(1):
                        k = i.r
                        dve.wait_ge(row_sum, i.count())
                        wait(dve, ne["sums"], i.count(4, per=3))
                        for b in range(GB):
                            dve.bn_stats(stats_e[k][:, b, :], ROW_I[:, b * N:(b + 1) * N])
                        for b in range(GB):
                            last = dve.bn_stats(stats_e[k][:, GB + b, :], ROW_J[:, b * N:(b + 1) * N])
                        last.then_inc(ne["stats"], 1)
                    if i := stage(3):
                        k = i.r
                        dve.wait_ge(n3["rstd"], i.count())
                        wait(dve, turned3, i.count(2))
                        normalise(dve, y3[k], x3[k], mean3[k], rstd3[k], y3_set)
                    if i := stage(2):
                        dve.wait_ge(weights_set, i.count())
                        wait(dve, values_set, i.count(2))
                        dve.reciprocal(inv[i.r], sums[i.r]).then_inc(inv_set, 1)
                    if i := stage(4):
                        low(i, u1_hi_set, o_sum, u1_lo[i.r], U1_BANK, u1_hi[i.r], u1_lo_set)
                    if i := stage(0):
                        k = i.r
                        dve.wait_ge(n2["rstd"], i.count())
                        wait(dve, turned2, i.count(4))
                        wait(dve, values_set, i.count(4))
                        normalise(dve, y2[k], x2[k], mean2[k], rstd2[k], y2_set)
                sweep(dve, G, U, 2, 5, body)

            @block.scalar
            def _(act):
                def high(i, summed, out_free, out, bank, done):
                    act.wait_ge(summed, i.count())
                    wait(act, out_free, i.count(2))
                    act.activation(out, bank, ACT.Copy).then_inc(done, 1)

                def body(stage):
                    if i := stage(0):
                        act.wait_ge(turned2, i.count())
                        wait(act, col_sum, i.count(4))
                        act.activation(h2[i.r], TURN2, ACT.Relu).then_inc(h2_set, 1)
                    if i := stage(3):
                        high(i, u2_sum, u1_sum, u2_hi[i.r], U2_BANK, u2_hi_set)
                    if i := stage(1):
                        k = i.r
                        act.wait_ge(nbias_set, i.count())
                        wait(act, inv_set, i.count(2))
                        for c in range(NK):
                            last = act.activation(scores[k][:, c, :], scores[k][:, c, :], ACT.Exp, bias=nbias[k][:, c:c + 1],
                                                  scale=graph[k][:, 2, c // NT:c // NT + 1], accum_out=sums[k][:, c:c + 1])
                        last.then_inc(weights_set, 1)
                    if i := stage(3):
                        high(i, u1_sum, o_sum, u1_hi[i.r], U1_BANK, u1_hi_set)
                    if i := stage(1):
                        k = i.r
                        act.wait_ge(inv_set, i.count())
                        wait(act, att_sum, i.count(2))
                        for t in range(NT):
                            for b in range(GB):
                                n, c = t * GB + b, b * NT + t
                                last = act.activation(values[k][:, n * D:(n + 1) * D], y2[k][:, n * D:(n + 1) * D],
                                                      ACT.Relu, scale=inv[k][:, c:c + 1])
                        last.then_inc(values_set, 1)
                    if i := stage(2):
                        act.wait_ge(turned3, i.count())
                        wait(act, o_sum, i.count(2))
                        act.activation(h3[i.r], TURN3, ACT.Relu).then_inc(h3_set, 1)
                    if i := stage(1):
                        act.wait_ge(att_sum, i.count())
                        wait(act, x3_set, i.count(2))
                        act.activation(att[i.r], ATT, ACT.Tanh, scale=0.5).then_inc(att_set, 1)
                    if i := stage(2):
                        high(i, v_sum, u2_sum, v_hi[i.r], V_BANK, v_hi_set)
                sweep(act, G, U, 2, 3, body)

            @block.tensor
            def _(pe):
                def body(stage):
                    if i := stage(0):
                        pe.wait_ge(h_landed[i.r], i.dma())
                        wait(pe, x2_set, i.count(1))
                        flip_back(pe, BACK, h_in[i.r], ident, back)
                    if i := stage(4):
                        pe.wait_ge(y3_set, i.count())
                        wait(pe, u2_lo_set, i.count(1))
                        flip(pe, TURN3, y3[i.r], ident, turned3)
                    if i := stage(5):
                        pe.wait_ge(u1_lo_set, i.count())
                        by_adjacency(pe, O_BANK, adj_hi, adj_lo, u1_hi[i.r], u1_lo[i.r]).then_inc(o_sum, 1)
                    if i := stage(3):
                        k = i.r
                        pe.wait_ge(values_set, i.count())
                        wait(pe, att_set, i.count(1))
                        first = True
                        for t in range(NT):
                            for b in range(GB):
                                n = t * GB + b
                                for j in range(NT):
                                    last = pe.matmul(ATT[:, n * D:(n + 1) * D], scores[k][:, b * NT + j, t * P:(t + 1) * P],
                                                     values[k][:, (j * GB + b) * D:(j * GB + b + 1) * D],
                                                     start=first, stop=False, skip_group_check=True)
                                    first = False
                        last.then_inc(att_sum, 1)
                    if i := stage(4):
                        pe.wait_ge(h3_set, i.count())
                        wait(pe, v_lo_set, i.count(1))
                        by_weight(pe, V_BANK, h3[i.r], cheb3[:, 3, :]).then_inc(v_sum, 1)
                    if i := stage(1):
                        pe.wait_ge(y2_set, i.count())
                        wait(pe, u1_lo_set, i.count(4))
                        wait(pe, h2_set, i.count(1))
                        flip(pe, TURN2, y2[i.r], ident, turned2)
                    if i := stage(4):
                        by_weight(pe, U2_BANK, h3[i.r], cheb3[:, 2, :])
                        wait(pe, u1_lo_set, i.count(1))
                        pe.wait_ge(h2_set, i.count(-3))
                        by_weight(pe, U1_BANK, h3[i.r], cheb3[:, 1, :])
                        pe.wait_ge(v_lo_set, i.count())
                        by_adjacency(pe, U2_BANK, adj_hi, adj_lo, v_hi[i.r], v_lo[i.r]).then_inc(u2_sum, 1)
                    if i := stage(1):
                        k = i.r
                        pe.wait_ge(h2_set, i.count())
                        wait(pe, f_set, i.count(1))
                        pe.matmul(ROW_I, att_rep[:, 0, :], h2[k], start=True, stop=True)
                        wait(pe, shift_set, i.count(1))
                        pe.matmul(ROW_J, att_rep[:, 1, :], h2[k], start=True, stop=True).then_inc(row_sum, 1)
                    if i := stage(4):
                        wait(pe, result_set, i.count(1))
                        by_weight(pe, O_BANK, h3[i.r], cheb3[:, 0, :])
                        pe.wait_ge(u2_lo_set, i.count())
                        by_adjacency(pe, U1_BANK, adj_hi, adj_lo, u2_hi[i.r], u2_lo[i.r]).then_inc(u1_sum, 1)
                    if i := stage(1):
                        pe.wait_ge(ne["stats"], i.count())
                        for c in range(NK):
                            last = pe.matmul(COL_J[:, c:c + 1], h2[i.r][:, c * P:(c + 1) * P], att_col[:, 1:2],
                                             start=(c == 0), stop=False, skip_group_check=True)
                        last.then_inc(col_sum, 1)
                sweep(pe, G, U, 2, 5, body)


_INS = ['x', 'adj', 'L0_gnn_Theta1', 'L0_gnn_bias', 'L1_gnn_w3_w', 'L1_gnn_w3_b', 'L1_gnn_u3_w', 'L1_gnn_u3_b',
        'L1_gnn_w4_w', 'L1_gnn_w4_b', 'L1_gnn_w5_w', 'L1_gnn_w5_b', 'L1_gnn_u5_w', 'L1_gnn_u5_b', 'L2_gnn_a',
        'L3_gnn_weight_1']
_OUTS = [((B, N, D), 'float32')]


def kernel(**inputs):
    import numpy as _np
    import concourse.bacc as _bacc
    from concourse import mybir as _mybir
    from concourse.bass_utils import run_bass_kernel_spmd as _run

    nc = _bacc.Bacc("TRN2", target_bir_lowering=False, num_devices=1)
    arrays, args = {}, []
    for name in _INS:
        a = _np.ascontiguousarray(inputs[name])
        arrays[f"in_{name}_dram"] = a
        args.append(nc.dram_tensor(f"in_{name}_dram", a.shape, _mybir.dt.from_np(a.dtype), kind="ExternalInput").ap())
    for i, (shape, dtype) in enumerate(_OUTS):
        dt = _mybir.dt.from_np(_np.dtype(dtype))
        args.append(nc.dram_tensor(f"out_{i}_dram", shape, dt, kind="ExternalOutput").ap())
    build(nc, *args)
    r = _run(nc, [arrays], core_ids=[0])
    return r.results[0]["out_0_dram"]
```

```python
from contextlib import ExitStack

import concourse.bass as bass
from concourse import mybir

F32 = mybir.dt.float32
F32R = mybir.dt.float32r
ALU = mybir.AluOpType
ACT = mybir.ActivationFunctionType
AX = mybir.AxisListType

P = 128
B, N, D = 32, 256, 128
NT = N // P
GB = 2
G = B // GB
NK = NT * GB
W = GB * N
STEPS = 5
ITEMS = STEPS * G
LN_EPS = 1e-5
ATT_EPS = 1e-14
LEAK = 0.2
LOW = 32
MINUS_HALF, HALF, QUARTER, EPS = range(4)


class Parts:
    pass


class Item:

    def __init__(self, q, r, unroll, items):
        self.q, self.r, self.u, self.items = q, r, unroll, items

    def count(self, ago=0, per=1):
        at = per * (self.r - ago + 1)
        if isinstance(self.q, int):
            return min(per * self.u * self.q + at, per * self.items)
        return self.q * (per * self.u) + at

    def dma(self, per=1):
        return self.q * (16 * per) + 16 * per

    def before(self, ago):
        r = self.r - ago
        q = self.q + r // self.u if r // self.u else self.q
        return None if isinstance(q, int) and q < 0 else Item(q, r % self.u, self.u, self.items)

    def index(self):
        return self.q * self.u + self.r


def place(eng, index):
    return index if isinstance(index, int) else eng.snap(index)


def wait(eng, sem, value):
    if not isinstance(value, int) or value > 0:
        eng.wait_ge(sem, value)


class Sweep:

    def __init__(self, eng, items, unroll, head, lag, body, tail=0):
        self.eng, self.items, self.u, self.body = eng, items, unroll, body
        self.head, self.tail = head, items // unroll - tail
        self.loop_start, self.loop_end, self.end = head * unroll, self.tail * unroll, items + lag

    def slot(self, q, j, bounded):
        def stage(behind):
            r = j - behind
            q_, r_ = q + r // self.u if r // self.u else q, r % self.u
            if bounded and not 0 <= self.u * q_ + r_ < self.items:
                return None
            return Item(q_, r_, self.u, self.items)
        return self.body(stage) or ()

    def parts(self, first, last):
        for s in range(first, last):
            yield from self.slot(s // self.u, s % self.u, True)
            yield

    def peeled(self, first, last):
        for _ in self.parts(first, last):
            pass

    def loop(self):
        with self.eng.Fori(self.head, self.tail, 1) as q:
            for j in range(self.u):
                for _ in self.slot(q, j, False):
                    pass


def hand_over(old, new, after):
    parts, k = new.parts(0, new.loop_start), 0
    for s in range(old.loop_end, old.end):
        old.peeled(s, s + 1)
        while k < len(after) and after[k] <= s:
            next(parts)
            k += 1
    for _ in parts:
        pass


def build(nc, x, adj, Theta1, bias0, w3_w, w3_b, u3_w, u3_b, w4_w, w4_b, w5_w, w5_b, u5_w, u5_b, att, weight_1, out):
    x_dram = x.rearrange("b (t p) f -> b p t f", p=P)
    out_dram = out.rearrange("b (t p) f -> b p t f", p=P)

    with ExitStack() as whole:
        def sb(name, shape, dt=F32, ctx=whole):
            return ctx.enter_context(nc.sbuf_tensor(name, shape, dt))

        def sem(name):
            return whole.enter_context(nc.semaphore(name))

        psum = whole.enter_context(nc.psum_tensor("psum", [P, 8, 512], F32))

        x_store = sb("x_store", [P, G, W])
        h_store = sb("h_store", [P, G, W])

        ident = sb("ident", [P, P])
        adj_tr = sb("adj_tr", [P, NT, N])
        adj_nat_hi, adj_nat_lo = sb("adj_nat_hi", [P, NT, N], F32R), sb("adj_nat_lo", [P, NT, N], F32R)
        adj_tr_hi, adj_tr_lo = sb("adj_tr_hi", [P, NT, N], F32R), sb("adj_tr_lo", [P, NT, N], F32R)
        cheb0 = sb("cheb0", [P, 3, P])
        cheb3 = sb("cheb3", [P, 4, P])
        gate_hi, gate_lo = sb("gate_hi", [P, 5, P], F32R), sb("gate_lo", [P, 5, P], F32R)
        gate_b = sb("gate_b", [P, 3])
        bias_pair, ones_pair = sb("bias_pair", [LOW + 1, W], F32R), sb("ones_pair", [LOW + 1, P], F32R)
        att_col = sb("att_col", [P, 2])
        att_rep = sb("att_rep", [P, 2, P])
        consts = sb("consts", [P, 4, NK])
        ones = sb("ones", [P, W])

        x_in_landed = [sem(f"x_in_landed{r}") for r in range(4)]
        x_stored = [sem(f"x_stored{r}") for r in range(4)]
        h_stored = [sem(f"h_stored{r}") for r in range(4)]

        with ExitStack() as region:
            first = layer0(nc, psum, sem, region, x_dram, x_store, h_store, x_in_landed, x_stored, h_stored, ident,
                           adj_nat_hi, adj_nat_lo, cheb0, ones_pair, bias_pair, consts)
        early = early_buffers(nc, whole)
        with ExitStack() as region:
            prep = prepare(nc, psum, sem, sb, region, ident, adj, adj_nat_hi, adj_nat_lo, adj_tr,
                           adj_tr_hi, adj_tr_lo, Theta1, cheb0, weight_1, cheb3, (w3_w, w4_w, w5_w, u3_w, u5_w),
                           gate_hi, gate_lo, (w3_b, w4_b, w5_b, u3_b, u5_b), gate_b, bias0, ones_pair,
                           bias_pair, att, att_col, att_rep, consts, ones)
        with ExitStack() as region:
            gated = layer1(nc, psum, sem, region, h_store, h_stored, ident, adj_tr_hi, adj_tr_lo, gate_hi, gate_lo, gate_b)
        late = late_buffers(nc, whole)
        last = layers23(nc, psum, sem, early, late, gated.h_new_set, x_store, h_store, out_dram, ident, adj_tr,
                        adj_tr_hi, adj_tr_lo, cheb3, att_col, att_rep, consts, ones)

        with nc.Block() as block:
            @block.sync
            def _(sp):
                cheb, att_cheb = first.sync(sp), last.sync(sp)
                prep.load_adj(sp)
                cheb.peeled(0, 1)
                prep.load_cheb(sp)
                cheb.peeled(1, 3)
                prep.load_rest(sp)
                cheb.peeled(3, cheb.loop_start)
                cheb.loop()
                cheb.peeled(cheb.loop_end, cheb.end)
                for k in range(len(x_stored)):
                    sp.wait_ge(x_stored[k], 16 * (G // len(x_stored)))
                for k in range(len(h_stored)):
                    sp.wait_ge(h_stored[k], 16 * (G // len(h_stored)))
                att_cheb.peeled(0, att_cheb.loop_start)
                sp.wait_ge(gated.h_new_set, ITEMS)
                att_cheb.loop()
                att_cheb.peeled(att_cheb.loop_end, att_cheb.end)
                last.all_stored(sp)

            @block.gpsimd
            def _(pool):
                cheb, gates, att_cheb = first.gpsimd(pool), gated.gpsimd(pool), last.gpsimd(pool)
                prep.gpsimd(pool)
                cheb.peeled(0, cheb.loop_start)
                cheb.loop()
                hand_over(cheb, gates, ())
                gates.loop()
                hand_over(gates, att_cheb, [67, 68, 68, 69, 70, 70, 73, 74])
                att_cheb.loop()
                att_cheb.peeled(att_cheb.loop_end, att_cheb.end)

            @block.vector
            def _(dve):
                cheb, gates, att_cheb = first.vector(dve), gated.vector(dve), last.vector(dve)
                prep.vector_ones(dve)
                cheb.peeled(0, 1)
                prep.vector_cheb(dve)
                cheb.peeled(1, 5)
                prep.vector_sums(dve)
                cheb.peeled(5, 7)
                prep.vector_turned(dve)
                cheb.peeled(7, 8)
                prep.vector_gate_lo(dve)
                cheb.loop()
                hand_over(cheb, gates, [G + 1, G + 2, G + 3])
                gates.loop()
                hand_over(gates, att_cheb, [69, 69, 70, 70, 71, 71, 71, 73, 74, 74, 80, 80, 80, 80])
                att_cheb.loop()
                att_cheb.peeled(att_cheb.loop_end, att_cheb.end)

            @block.scalar
            def _(act):
                cheb, gates, att_cheb = first.scalar(act), gated.scalar(act), last.scalar(act)
                prep.scalar_cheb(act)
                cheb.peeled(0, 4)
                prep.scalar_adj_tr(act)
                cheb.peeled(4, 6)
                prep.scalar_gates(act)
                cheb.peeled(6, cheb.loop_start)
                cheb.loop()
                hand_over(cheb, gates, [G, G + 1, G + 2, G + 3])
                gates.loop()
                hand_over(gates, att_cheb, [72, 72])
                att_cheb.loop()
                att_cheb.peeled(att_cheb.loop_end, att_cheb.end)

            @block.tensor
            def _(pe):
                cheb, gates, att_cheb = first.tensor(pe), gated.tensor(pe), last.tensor(pe)
                prep.tensor_adj(pe)
                cheb.peeled(0, 4)
                prep.tensor_gates(pe)
                cheb.peeled(4, cheb.loop_start)
                cheb.loop()
                prep.wait_gates(pe)
                hand_over(cheb, gates, [G, G + 1, G + 2, G + 3])
                gates.loop()
                hand_over(gates, att_cheb, [69, 69, 69, 69, 69, 70, 71, 72, 73, 73, 74, 76, 76])
                att_cheb.loop()
                att_cheb.peeled(att_cheb.loop_end, att_cheb.end)


def prepare(nc, psum, sem, sb, region, ident, adj, adj_nat_hi, adj_nat_lo, adj_tr, adj_tr_hi, adj_tr_lo,
            Theta1, cheb0, weight_1, cheb3, weights, gate_hi, gate_lo,
            biases, gate_b, bias0, ones_pair, bias_pair, att, att_col, att_rep, consts, ones):
    w3_w, w4_w, w5_w, u3_w, u5_w = weights
    adj_nat = sb("adj_nat", [P, NT, N], F32, region)
    theta = sb("theta", [P, 5, P], F32, region)
    cheb_raw = sb("cheb_raw", [P, P, 7], F32, region)
    gate_raw = sb("gate_raw", [P, 8, P], F32, region)
    gate_sum, gate_w = sb("gate_sum", [P, 5, P], F32, region), sb("gate_w", [P, 5, P], F32, region)
    bias_raw = sb("bias_raw", [P, 5], F32, region)
    bias_one, bias_row = sb("bias_one", [LOW + 1, P], F32, region), sb("bias_row", [LOW + 1, W], F32, region)
    adj_loaded, cheb_loaded, loaded = sem("adj_loaded"), sem("cheb_loaded"), sem("loaded")
    zeroed, ident_set, consts_set, ones_set = sem("zeroed"), sem("ident_set"), sem("consts_set"), sem("ones_set")
    adj_turned, adj_tr_set, adj_split, adj_hi_set = sem("adj_turned"), sem("adj_tr_set"), sem("adj_split"), sem("adj_hi_set")
    summed, turned, gate_set, gate_hi_set, w34 = sem("summed"), sem("turned"), sem("gate_set"), sem("gate_hi_set"), sem("w34")
    cheb_part, blank, row_set, row_hi, row_lo, rest_set = (
        sem(n) for n in ("cheb_part", "blank", "row_set", "row_hi", "row_lo", "rest_set"))
    ADJ_BANK, GATE_BANK, LAST_GATE_BANK = (psum[:, k] for k in (5, 0, 2))
    LOADS = 16 * (6 + 5 + 2)
    REST = 4 + 3 + 2

    def load_adj(sp):
        sp.dma_start(adj_nat[:], adj.rearrange("(t p) w -> p t w", p=P)).then_inc(adj_loaded, 16)

    def load_cheb(sp):
        sp.dma_start(theta[:], Theta1.rearrange("(k f) o -> f k o", f=P)).then_inc(cheb_loaded, 16)
        sp.wait_ge(blank, 1)
        for row in (0, LOW):
            sp.dma_start(bias_one[row:row + 1, :], bias0.rearrange("(o f) -> o f", o=1)).then_inc(cheb_loaded, 16)

    def load_rest(sp):
        sp.dma_start(gate_raw[:, 0:2, :], w4_w.rearrange("o (c i) -> o c i", i=P)).then_inc(loaded, 16)
        sp.dma_start(gate_raw[:, 2:4, :], w3_w.rearrange("o (c i) -> o c i", i=P)).then_inc(loaded, 16)
        sp.dma_start(gate_raw[:, 4:6, :], w5_w.rearrange("o (c i) -> o c i", i=P)).then_inc(loaded, 16)
        sp.dma_start(gate_raw[:, 6, :], u3_w).then_inc(loaded, 16)
        sp.dma_start(gate_raw[:, 7, :], u5_w).then_inc(loaded, 16)
        sp.dma_start(cheb_raw[:], weight_1).then_inc(loaded, 16)
        for k, b in enumerate(biases):
            sp.dma_start(bias_raw[:, k:k + 1], b.rearrange("(p o) -> p o", o=1)).then_inc(loaded, 16)
        for k in range(2):
            sp.dma_start(att_col[:, k:k + 1], att[k * D:(k + 1) * D, :]).then_inc(loaded, 16)

    def gpsimd(pool):
        pool.memset(ident[:], 0.0).then_inc(zeroed, 1)
        pool.wait_ge(zeroed, 1)
        pool.affine_select(out=ident[:], in_=ident[:], compare_op=ALU.not_equal, fill=1.0, base=0,
                           pattern=[[-1, P]], channel_multiplier=1).then_inc(ident_set, 1)
        for which, value in ((MINUS_HALF, -0.5), (HALF, 0.5), (QUARTER, 0.25), (EPS, ATT_EPS)):
            pool.memset(consts[:, which], value).then_inc(consts_set, 1)
        pool.wait_ge(consts_set, 4)
        pool.wait_ge(ones_set, 1)

    def vector_ones(dve):
        dve.memset(bias_one[:], 0.0).then_inc(blank, 1)
        dve.memset(ones[:], 1.0).then_inc(ones_set, 1)

    def vector_cheb(dve):
        dve.wait_ge(adj_loaded, 16)
        dve.wait_ge(adj_hi_set, 1)
        dve.tensor_tensor(adj_nat_lo[:], adj_nat[:], adj_nat_hi[:].bitcast(F32), ALU.subtract).then_inc(adj_split, 1)
        dve.wait_ge(cheb_loaded, 48)
        for k in range(NK):
            dve.tensor_copy(bias_row[:, k * P:(k + 1) * P], bias_one[:]).then_inc(row_set, 1)
        dve.tensor_tensor(cheb0[:, 1, :], theta[:, 1, :], theta[:, 3, :], ALU.add).then_inc(cheb_part, 1)
        dve.tensor_tensor(cheb0[:, 2, :], theta[:, 2, :], theta[:, 4, :], ALU.add).then_inc(cheb_part, 1)
        dve.wait_ge(cheb_part, 2)
        dve.tensor_tensor(cheb0[:, 0, :], theta[:, 0, :], cheb0[:, 2, :], ALU.subtract).then_inc(cheb_part, 1)
        dve.wait_ge(cheb_part, 3)
        dve.tensor_scalar(cheb0[:, 2, :], cheb0[:, 2, :], 2.0, None, ALU.mult).then_inc(cheb_part, 1)
        dve.wait_ge(ones_set, 1)
        dve.tensor_copy(ones_pair[:], ones[0:LOW + 1, 0:P]).then_inc(cheb_part, 1)
        dve.wait_ge(row_hi, 1)
        dve.tensor_tensor(bias_pair[LOW:LOW + 1, :], bias_row[LOW:LOW + 1, :], bias_pair[LOW:LOW + 1, :].bitcast(F32),
                          ALU.subtract).then_inc(row_lo, 1)

    def vector_sums(dve):
        dve.wait_ge(adj_turned, 1)
        dve.tensor_copy(adj_tr[:].rearrange("p t n -> p (t n)"), ADJ_BANK).then_inc(adj_tr_set, 1)
        dve.wait_ge(loaded, LOADS)
        halves = gate_raw[:, 0:6, :].rearrange("p (k c) i -> p k c i", c=2)
        dve.tensor_tensor(gate_sum[:, 0:3, :], halves[:, :, 0, :], halves[:, :, 1, :], ALU.add).then_inc(summed, 1)
        dve.tensor_copy(gate_sum[:, 3:5, :], gate_raw[:, 6:8, :]).then_inc(summed, 1)
        dve.tensor_copy(cheb3[:, 0, :], cheb_raw[:, :, 0]).then_inc(rest_set, 1)
        for k in range(1, 4):
            dve.tensor_tensor(cheb3[:, k, :], cheb_raw[:, :, k], cheb_raw[:, :, k + 3], ALU.add).then_inc(rest_set, 1)
        for k, other in ((0, 1), (1, 0), (2, 2)):
            dve.tensor_tensor(gate_b[:, k:k + 1], bias_raw[:, other:other + 1],
                              bias_raw[:, 3 + k // 2:4 + k // 2], ALU.add).then_inc(rest_set, 1)
        for k in range(2):
            dve.tensor_scalar(att_rep[:, k, :], ones[:, 0:P], att_col[:, k:k + 1], None, ALU.mult).then_inc(rest_set, 1)

    def vector_turned(dve):
        dve.wait_ge(adj_hi_set, 2)
        dve.wait_ge(adj_tr_set, 1)
        dve.tensor_tensor(adj_tr_lo[:], adj_tr[:], adj_tr_hi[:].bitcast(F32), ALU.subtract).then_inc(adj_split, 1)
        dve.wait_ge(turned, 1)
        dve.tensor_copy(gate_w[:, 0:4, :].rearrange("p k o -> p (k o)"), GATE_BANK).then_inc(gate_set, 1)
        dve.tensor_copy(gate_w[:, 4, :], LAST_GATE_BANK[:, 0:P]).then_inc(gate_set, 1)
        dve.wait_ge(gate_set, 2)
        dve.tensor_tensor(gate_w[:, 1, :], gate_w[:, 1, :], gate_w[:, 0, :], ALU.subtract).then_inc(w34, 1)

    def vector_gate_lo(dve):
        dve.wait_ge(gate_hi_set, 1)
        dve.tensor_tensor(gate_lo[:], gate_w[:], gate_hi[:].bitcast(F32), ALU.subtract).then_inc(gate_set, 1)

    def scalar_cheb(act):
        act.wait_ge(adj_loaded, 16)
        act.activation(adj_nat_hi[:], adj_nat[:], ACT.Copy).then_inc(adj_hi_set, 1)
        act.wait_ge(row_set, NK)
        act.activation(bias_pair[:], bias_row[:], ACT.Copy).then_inc(row_hi, 1)

    def scalar_adj_tr(act):
        act.wait_ge(adj_tr_set, 1)
        act.activation(adj_tr_hi[:], adj_tr[:], ACT.Copy).then_inc(adj_hi_set, 1)

    def scalar_gates(act):
        act.wait_ge(w34, 1)
        act.activation(gate_hi[:], gate_w[:], ACT.Copy).then_inc(gate_hi_set, 1)
        act.wait_ge(rest_set, REST)

    def tensor_adj(pe):
        pe.wait_ge(ident_set, 1)
        pe.wait_ge(adj_loaded, 16)
        for t in range(NT):
            for u in range(NT):
                last = pe.transpose(ADJ_BANK[:, (u * NT + t) * P:(u * NT + t + 1) * P],
                                    adj_nat[:, t, u * P:(u + 1) * P], ident[:])
        last.then_inc(adj_turned, 1)
        pe.wait_ge(cheb_part, 5)
        pe.wait_ge(row_lo, 1)
        pe.wait_ge(adj_split, 1)

    def tensor_gates(pe):
        pe.wait_ge(summed, 2)
        for k in range(5):
            bank = GATE_BANK if k < 4 else LAST_GATE_BANK
            last = pe.transpose(bank[:, (k % 4) * P:(k % 4 + 1) * P], gate_sum[:, k, :], ident[:])
        last.then_inc(turned, 1)

    def wait_gates(pe):
        pe.wait_ge(gate_set, 3)
        pe.wait_ge(adj_split, 2)
        pe.wait_ge(rest_set, REST)

    parts = Parts()
    parts.load_adj = load_adj
    parts.load_cheb = load_cheb
    parts.load_rest = load_rest
    parts.gpsimd = gpsimd
    parts.vector_ones = vector_ones
    parts.vector_cheb = vector_cheb
    parts.vector_sums = vector_sums
    parts.vector_turned = vector_turned
    parts.vector_gate_lo = vector_gate_lo
    parts.scalar_cheb = scalar_cheb
    parts.scalar_adj_tr = scalar_adj_tr
    parts.scalar_gates = scalar_gates
    parts.tensor_adj = tensor_adj
    parts.tensor_gates = tensor_gates
    parts.wait_gates = wait_gates
    return parts


def norm_sems(sem, name):
    return {k: sem(f"{name}_{k}") for k in ("stats", "sums", "scaled", "quarter", "var", "rstd")}


def norm_stats(dve, s, stats, tile, width):
    for k in range(NK):
        last = dve.bn_stats(stats[:, k, :], tile[:, k * width:(k + 1) * width])
    last.then_inc(s["stats"], 1)


def variance(pool, s, item, stats, work, mean, count, eps, consts, half=0.5):
    mean_e, m2_e, mean_o, m2_o = (stats[:, :, k] for k in (1, 2, 4, 5))
    total, diff, dev, square = (work[:, k, :] for k in range(4))
    pool.wait_ge(s["stats"], item.count())
    pool.tensor_tensor(total, mean_e, mean_o, ALU.add).then_inc(s["sums"], 1)
    pool.tensor_tensor(diff, mean_e, mean_o, ALU.subtract).then_inc(s["sums"], 1)
    pool.tensor_tensor(dev, m2_e, m2_o, ALU.add).then_inc(s["sums"], 1)
    pool.wait_ge(s["sums"], item.count(per=3))
    pool.tensor_tensor(square, diff, diff, ALU.mult).then_inc(s["scaled"], 1)
    pool.tensor_scalar(mean, total, half, 0.0, ALU.mult, ALU.add).then_inc(s["scaled"], 1)
    pool.tensor_scalar(dev, dev, 1.0 / count, eps, ALU.mult, ALU.add).then_inc(s["scaled"], 1)
    pool.wait_ge(s["scaled"], item.count(per=3))
    pool.tensor_tensor(square, square, consts[:, QUARTER], ALU.mult).then_inc(s["quarter"], 1)
    pool.wait_ge(s["quarter"], item.count())
    pool.tensor_tensor(dev, dev, square, ALU.add).then_inc(s["var"], 1)
    return dev


def norm_scalars(pool, s, item, stats, work, mean, rstd, consts, half=0.5):
    dev = variance(pool, s, item, stats, work, mean, D, LN_EPS, consts, half)
    pool.wait_ge(s["var"], item.count())
    pool.tensor_tensor(rstd, dev, consts[:, MINUS_HALF], ALU.pow).then_inc(s["rstd"], 1)


def normalise(dve, tile, source, mean, rstd, done):
    for k in range(NK):
        last = dve.tensor_scalar(tile[:, k * D:(k + 1) * D], source[:, k * D:(k + 1) * D],
                                 mean[:, k:k + 1], rstd[:, k:k + 1], ALU.subtract, ALU.mult)
    last.then_inc(done, 1)


def flip(pe, bank, tile, ident, done):
    for t in range(NT):
        for b in range(GB):
            k, c = t * GB + b, b * NT + t
            last = pe.transpose(bank[:, c * P:(c + 1) * P], tile[:, k * P:(k + 1) * P], ident[:])
    last.then_inc(done, 1)


def flip_back(pe, bank, tile, ident, done):
    for t in range(NT):
        for b in range(GB):
            k, c = t * GB + b, b * NT + t
            last = pe.transpose(bank[:, k * P:(k + 1) * P], tile[:, c * P:(c + 1) * P], ident[:])
    last.then_inc(done, 1)


def by_weight(pe, bank, h_feat, weight):
    for t in range(NT):
        for b in range(GB):
            k, c = t * GB + b, b * NT + t
            last = pe.matmul(bank[:, k * P:(k + 1) * P], h_feat[:, c * P:(c + 1) * P], weight,
                             start=(k == 0), stop=False, skip_group_check=True)
    return last


def by_adjacency(pe, bank, mat_hi, mat_lo, v_hi, v_lo):
    for n in range(NT):
        for m in range(NT):
            for left, right in ((mat_hi, v_hi), (mat_hi, v_lo), (mat_lo, v_hi)):
                last = pe.matmul(bank[:, n * GB * D:(n + 1) * GB * D], left[:, m, n * P:(n + 1) * P],
                                 right[:, m * GB * D:(m + 1) * GB * D], start=False, stop=False, skip_group_check=True)
    return last


def layer0(nc, psum, sem, region, x_dram, x_store, h_store, x_in_landed, x_stored, h_stored, ident,
           adj_hi, adj_lo, cheb0, ones_pair, bias_pair, consts):
    U = 4
    def ring(name, n, shape=(W,), dt=F32):
        t = region.enter_context(nc.sbuf_tensor("l0_" + name, [P, n, *shape], dt))
        return [t[:, k] for k in range(n)]

    x_in, x_new = ring("x_in", 4), ring("x_new", 4)
    y, y_new = ring("y", 2), ring("y_new", 2)
    h_feat, h_next = ring("h_feat", 2), ring("h_next", 4)
    v_hi, v_lo = ring("v_hi", 2, dt=F32R), ring("v_lo", 2, dt=F32R)
    u_hi, u_lo = ring("u_hi", 2, dt=F32R), ring("u_lo", 2, dt=F32R)
    stats, stats_new = ring("stats", 2, (NK, 6)), ring("stats_new", 2, (NK, 6))
    work, work_new = ring("work", 2, (4, NK)), ring("work_new", 2, (4, NK))
    mean, rstd = ring("mean", 2, (NK,)), ring("rstd", 2, (NK,))
    mean_new, rstd_new = ring("mean_new", 2, (NK,)), ring("rstd_new", 2, (NK,))
    n_in, n_out = norm_sems(sem, "l0_in"), norm_sems(sem, "l0_out")
    y_set, y_new_set = sem("l0_y_set"), sem("l0_y_new_set")
    turned, turned_new = sem("l0_turned"), sem("l0_turned_new")
    h_set, h_next_set = sem("l0_h_set"), sem("l0_h_next_set")
    v_sum, v_hi_set, v_lo_set = sem("l0_v_sum"), sem("l0_v_hi_set"), sem("l0_v_lo_set")
    u_sum, u_hi_set, u_lo_set = sem("l0_u_sum"), sem("l0_u_hi_set"), sem("l0_u_lo_set")
    o_sum, x_new_set = sem("l0_o_sum"), sem("l0_x_new_set")
    T_BANK, T_NEW_BANK, V_BANK, U_BANK, O_BANK = (psum[:, k] for k in (1, 3, 6, 4, 7))

    def sync(sp):
        def body(stage):
            if i := stage(0):
                at = place(sp, i.index())
                wait(sp, x_new_set, i.count(4))
                for b in range(GB):
                    sp.dma_start(x_in[i.r].rearrange("p (t b f) -> p b t f", t=NT, b=GB)[:, b],
                                 x_dram[at * GB + b]).then_inc(x_in_landed[i.r], 16)
            if i := stage(7):
                at = place(sp, i.index())
                sp.wait_ge(x_new_set, i.count())
                sp.wait_ge(h_next_set, i.count())
                sp.dma_start(x_store[:, at], x_new[i.r]).then_inc(x_stored[i.r], 16)
                sp.dma_start(h_store[:, at], h_next[i.r]).then_inc(h_stored[i.r], 16)
        return Sweep(sp, G, U, 2, 7, body)

    def gpsimd(pool):
        def body(stage):
            if i := stage(0):
                wait(pool, y_set, i.count(2))
                norm_scalars(pool, n_in, i, stats[i.r % 2], work[i.r % 2], mean[i.r % 2], rstd[i.r % 2], consts)
            if i := stage(3):
                wait(pool, y_new_set, i.count(2))
                norm_scalars(pool, n_out, i, stats_new[i.r % 2], work_new[i.r % 2], mean_new[i.r % 2],
                             rstd_new[i.r % 2], consts)
        return Sweep(pool, G, U, 2, 3, body)

    def vector(dve):
        def body(stage):
            if i := stage(0):
                dve.wait_ge(x_in_landed[i.r], i.dma(per=GB))
                wait(dve, n_in["sums"], i.count(2, per=3))
                norm_stats(dve, n_in, stats[i.r % 2], x_in[i.r], D)
            if i := stage(1):
                dve.wait_ge(n_in["rstd"], i.count())
                wait(dve, turned, i.count(2))
                normalise(dve, y[i.r % 2], x_in[i.r], mean[i.r % 2], rstd[i.r % 2], y_set)
            if i := stage(2):
                dve.wait_ge(v_hi_set, i.count())
                wait(dve, u_sum, i.count(2))
                dve.tensor_tensor(v_lo[i.r % 2], V_BANK, v_hi[i.r % 2].bitcast(F32), ALU.subtract).then_inc(v_lo_set, 1)
            if i := stage(3):
                dve.wait_ge(o_sum, i.count())
                if not isinstance(i.q, int) or i.q > 0:
                    dve.wait_ge(x_stored[i.r], i.q * 16)
                dve.scalar_tensor_tensor(x_new[i.r], O_BANK, 0.0, x_in[i.r], ALU.max, ALU.add).then_inc(x_new_set, 1)
                dve.wait_ge(x_new_set, i.count())
                wait(dve, n_out["sums"], i.count(2, per=3))
                norm_stats(dve, n_out, stats_new[i.r % 2], x_new[i.r], D)
            if i := stage(4):
                dve.wait_ge(n_out["rstd"], i.count())
                wait(dve, turned_new, i.count(2))
                normalise(dve, y_new[i.r % 2], x_new[i.r], mean_new[i.r % 2], rstd_new[i.r % 2], y_new_set)
            if i := stage(2):
                dve.wait_ge(u_hi_set, i.count())
                wait(dve, o_sum, i.count(2))
                dve.tensor_tensor(u_lo[i.r % 2], U_BANK, u_hi[i.r % 2].bitcast(F32), ALU.subtract).then_inc(u_lo_set, 1)
        return Sweep(dve, G, U, 2, 4, body)

    def scalar(act):
        def body(stage):
            if i := stage(0):
                act.wait_ge(turned, i.count())
                wait(act, o_sum, i.count(2))
                act.activation(h_feat[i.r % 2], T_BANK, ACT.Relu).then_inc(h_set, 1)
            if i := stage(1):
                act.wait_ge(u_sum, i.count())
                wait(act, o_sum, i.count(2))
                act.activation(u_hi[i.r % 2], U_BANK, ACT.Copy).then_inc(u_hi_set, 1)
            if i := stage(0):
                act.wait_ge(v_sum, i.count())
                wait(act, u_sum, i.count(2))
                act.activation(v_hi[i.r % 2], V_BANK, ACT.Copy).then_inc(v_hi_set, 1)
            if i := stage(4):
                act.wait_ge(turned_new, i.count())
                if not isinstance(i.q, int) or i.q > 0:
                    act.wait_ge(h_stored[i.r], i.q * 16)
                act.activation(h_next[i.r], T_NEW_BANK, ACT.Relu).then_inc(h_next_set, 1)
        return Sweep(act, G, U, 2, 4, body)

    def tensor(pe):
        def body(stage):
            if i := stage(0):
                pe.wait_ge(y_set, i.count())
                wait(pe, h_set, i.count(1))
                flip(pe, T_BANK, y[i.r % 2], ident, turned)
            if i := stage(1):
                pe.wait_ge(v_lo_set, i.count())
                by_adjacency(pe, U_BANK, adj_hi, adj_lo, v_hi[i.r % 2], v_lo[i.r % 2]).then_inc(u_sum, 1)
                wait(pe, x_new_set, i.count(1))
                by_weight(pe, O_BANK, h_feat[i.r % 2], cheb0[:, 0, :])
                pe.matmul(O_BANK, ones_pair[:], bias_pair[:], start=False, stop=False, skip_group_check=True)
            if i := stage(0):
                pe.wait_ge(h_set, i.count())
                wait(pe, v_lo_set, i.count(1))
                by_weight(pe, V_BANK, h_feat[i.r % 2], cheb0[:, 2, :]).then_inc(v_sum, 1)
            if i := stage(1):
                pe.wait_ge(u_lo_set, i.count())
                by_adjacency(pe, O_BANK, adj_hi, adj_lo, u_hi[i.r % 2], u_lo[i.r % 2]).then_inc(o_sum, 1)
            if i := stage(0):
                wait(pe, u_lo_set, i.count(1))
                by_weight(pe, U_BANK, h_feat[i.r % 2], cheb0[:, 1, :])
            if i := stage(4):
                pe.wait_ge(y_new_set, i.count())
                wait(pe, h_next_set, i.count(1))
                flip(pe, T_NEW_BANK, y_new[i.r % 2], ident, turned_new)
        return Sweep(pe, G, U, 2, 4, body)

    parts = Parts()
    parts.sync, parts.gpsimd, parts.vector, parts.scalar, parts.tensor = sync, gpsimd, vector, scalar, tensor
    return parts


def layer1(nc, psum, sem, region, h_store, h_stored, ident, adj_hi, adj_lo, gate_hi, gate_lo, gate_b):
    U = G
    W4, W34, W5, U3, U5 = range(5)
    def ring(name, n, dt=F32):
        t = region.enter_context(nc.sbuf_tensor("l1_" + name, [P, n, W], dt))
        return [t[:, k] for k in range(n)]

    h = [h_store[:, g] for g in range(G)]
    h_hi, h_lo = ring("h_hi", 2, F32R), ring("h_lo", 2, F32R)
    ht_hi, ht_lo = ring("ht_hi", 2, F32R), ring("ht_lo", 2, F32R)
    m_hi, m_lo = ring("m_hi", 2, F32R), ring("m_lo", 2, F32R)
    r_gate, z_gate, rh, cand = ring("r_gate", 2), ring("z_gate", 2), ring("rh", 2), ring("cand", 2)
    rh_hi, rh_lo = ring("rh_hi", 2, F32R), ring("rh_lo", 2, F32R)
    step, zstep = ring("step", 2), ring("zstep", 2)
    names = ("turned", "ht_hi_set", "ht_lo_set", "h_hi_set", "h_lo_set", "m_sum", "m_hi_set", "m_lo_set", "r_sum",
             "r_set", "z_sum", "z_set", "rh_set", "rh_hi_set", "rh_lo_set", "c_sum", "c_set", "step_set",
             "zstep_set", "h_new_set")
    (turned, ht_hi_set, ht_lo_set, h_hi_set, h_lo_set, m_sum, m_hi_set, m_lo_set, r_sum, r_set, z_sum, z_set,
     rh_set, rh_hi_set, rh_lo_set, c_sum, c_set, step_set, zstep_set, h_new_set) = (sem("l1_" + n) for n in names)
    T_BANK, M_BANK, RZ_BANK, C_BANK = (psum[:, k] for k in (0, 2, 5, 6))

    def first_h(eng, i):
        if isinstance(i.q, int) and i.q == 0:
            eng.wait_ge(h_stored[i.r % len(h_stored)], 16 * (i.r // len(h_stored) + 1))

    def gpsimd(pool):
        def body(stage):
            if i := stage(1):
                k = i.r % 2
                pool.wait_ge(step_set, i.count())
                pool.wait_ge(z_set, i.count())
                wait(pool, h_new_set, i.count(2))
                pool.tensor_tensor(zstep[k], z_gate[k], step[k], ALU.mult).then_inc(zstep_set, 1)
            if i := stage(0):
                k = i.r % 2
                pool.wait_ge(c_set, i.count())
                wait(pool, zstep_set, i.count(2))
                pool.tensor_tensor(step[k], cand[k], h[i.r], ALU.subtract).then_inc(step_set, 1)
        return Sweep(pool, ITEMS, U, 1, 1, body, tail=1)

    def vector(dve):
        def body(stage):
            if i := stage(0):
                k = i.r % 2
                dve.wait_ge(ht_hi_set, i.count())
                wait(dve, m_sum, i.count(2))
                dve.tensor_tensor(ht_lo[k], T_BANK, ht_hi[k].bitcast(F32), ALU.subtract).then_inc(ht_lo_set, 1)
            if i := stage(3):
                k = i.r % 2
                dve.wait_ge(zstep_set, i.count())
                dve.tensor_tensor(h[i.r], h[i.r], zstep[k], ALU.add).then_inc(h_new_set, 1)
            if i := stage(1):
                k = i.r % 2
                dve.wait_ge(r_set, i.count())
                wait(dve, rh_lo_set, i.count(2))
                dve.tensor_tensor(rh[k], r_gate[k], h[i.r], ALU.mult).then_inc(rh_set, 1)
            if i := stage(0):
                k = i.r % 2
                dve.wait_ge(h_hi_set, i.count())
                wait(dve, r_sum, i.count(2))
                dve.tensor_tensor(h_lo[k], h[i.r], h_hi[k].bitcast(F32), ALU.subtract).then_inc(h_lo_set, 1)
            if i := stage(0):
                k = i.r % 2
                dve.wait_ge(m_hi_set, i.count())
                wait(dve, c_sum, i.count(2))
                dve.tensor_tensor(m_lo[k], M_BANK, m_hi[k].bitcast(F32), ALU.subtract).then_inc(m_lo_set, 1)
            if i := stage(1):
                k = i.r % 2
                dve.wait_ge(rh_hi_set, i.count())
                wait(dve, c_sum, i.count(2))
                dve.tensor_tensor(rh_lo[k], rh[k], rh_hi[k].bitcast(F32), ALU.subtract).then_inc(rh_lo_set, 1)
        return Sweep(dve, ITEMS, U, 1, 3, body, tail=1)

    def scalar(act):
        def body(stage):
            if i := stage(0):
                k = i.r % 2
                act.wait_ge(turned, i.count())
                wait(act, m_sum, i.count(2))
                act.activation(ht_hi[k], T_BANK, ACT.Copy).then_inc(ht_hi_set, 1)
            if i := stage(0):
                k = i.r % 2
                first_h(act, i)
                wait(act, h_new_set, i.count(G))
                wait(act, r_sum, i.count(2))
                act.activation(h_hi[k], h[i.r], ACT.Copy).then_inc(h_hi_set, 1)
            if i := stage(1):
                k = i.r % 2
                act.wait_ge(r_sum, i.count())
                wait(act, rh_set, i.count(2))
                act.activation(r_gate[k], RZ_BANK, ACT.Sigmoid, bias=gate_b[:, 0:1]).then_inc(r_set, 1)
            if i := stage(2):
                k = i.r % 2
                act.wait_ge(c_sum, i.count())
                wait(act, step_set, i.count(2))
                act.activation(cand[k], C_BANK, ACT.Tanh, bias=gate_b[:, 2:3]).then_inc(c_set, 1)
            if i := stage(1):
                k = i.r % 2
                act.wait_ge(rh_set, i.count())
                wait(act, c_sum, i.count(2))
                act.activation(rh_hi[k], rh[k], ACT.Copy).then_inc(rh_hi_set, 1)
            if i := stage(0):
                k = i.r % 2
                act.wait_ge(m_sum, i.count())
                wait(act, c_sum, i.count(2))
                act.activation(m_hi[k], M_BANK, ACT.Copy).then_inc(m_hi_set, 1)
            if i := stage(1):
                k = i.r % 2
                act.wait_ge(z_sum, i.count())
                wait(act, zstep_set, i.count(2))
                act.activation(z_gate[k], RZ_BANK, ACT.Sigmoid, bias=gate_b[:, 1:2]).then_inc(z_set, 1)
        return Sweep(act, ITEMS, U, 1, 2, body, tail=1)

    def tensor(pe):
        def gate(bank, which, v_hi, v_lo, start, stop):
            w_hi, w_lo = gate_hi[:, which, :], gate_lo[:, which, :]
            for n, (w, v) in enumerate(((w_hi, v_hi), (w_hi, v_lo), (w_lo, v_hi))):
                last = pe.matmul(bank, w, v, start=start and n == 0, stop=stop and n == 2, skip_group_check=True)
            return last

        def body(stage):
            if i := stage(0):
                k = i.r % 2
                first_h(pe, i)
                wait(pe, h_new_set, i.count(G))
                wait(pe, ht_lo_set, i.count(1))
                flip_back(pe, T_BANK, h[i.r], ident, turned)
            if i := stage(1):
                k = i.r % 2
                pe.wait_ge(h_lo_set, i.count())
                wait(pe, z_set, i.count(1))
                gate(RZ_BANK, U3, h_hi[k], h_lo[k], True, False)
            if i := stage(1):
                k = i.r % 2
                pe.wait_ge(m_lo_set, i.count())
                gate(RZ_BANK, W4, m_hi[k], m_lo[k], False, False).then_inc(r_sum, 1)
            if i := stage(2):
                k = i.r % 2
                pe.wait_ge(rh_lo_set, i.count())
                gate(C_BANK, U5, rh_hi[k], rh_lo[k], False, True).then_inc(c_sum, 1)
            if i := stage(0):
                k = i.r % 2
                pe.wait_ge(ht_lo_set, i.count())
                wait(pe, m_lo_set, i.count(1))
                for b in range(GB):
                    n = 0
                    for t in range(NT):
                        c = (t * GB + b) * P
                        for v, a in ((ht_hi, adj_hi), (ht_hi, adj_lo), (ht_lo, adj_hi)):
                            last = pe.matmul(M_BANK[:, b * N:(b + 1) * N], v[k][:, c:c + P], a[:, t, :],
                                             start=(b == 0 and n == 0), stop=False, skip_group_check=True)
                            n += 1
                last.then_inc(m_sum, 1)
            if i := stage(1):
                k = i.r % 2
                pe.wait_ge(r_set, i.count())
                gate(RZ_BANK, W34, m_hi[k], m_lo[k], False, True).then_inc(z_sum, 1)
            if i := stage(1):
                k = i.r % 2
                wait(pe, c_set, i.count(1))
                gate(C_BANK, W5, m_hi[k], m_lo[k], True, False)
        return Sweep(pe, ITEMS, U, 1, 2, body, tail=1)

    parts = Parts()
    parts.gpsimd, parts.vector, parts.scalar, parts.tensor = gpsimd, vector, scalar, tensor
    parts.h_new_set = h_new_set
    return parts


def ring_of_four(nc, ctx, name, n, shape=(W,), dt=F32):
    t = ctx.enter_context(nc.sbuf_tensor("l2_" + name, [P, n, *shape], dt))
    return [t[:, k % n] for k in range(4)]


def early_buffers(nc, ctx):
    def rings(names, n, shape=(W,)):
        return (ring_of_four(nc, ctx, name, n, shape) for name in names)

    early = Parts()
    early.scores = ring_of_four(nc, ctx, "scores", 2, (NK, N))
    early.x_in, early.h_in, early.att, early.values, early.h3 = rings(("x_in", "h_in", "att", "values", "h3"), 2)
    early.x2, early.y2, early.h2 = rings(("x2", "y2", "h2"), 4)
    early.shift, early.top, early.nbias, early.sums, early.inv = rings(("shift", "top", "nbias", "sums", "inv"), 2, (NK,))
    early.stats2, early.stats_e, early.stats3 = rings(("stats2", "stats_e", "stats3"), 4, (NK, 6))
    early.work2, early.work_e, early.work3 = rings(("work2", "work_e", "work3"), 4, (4, NK))
    early.mean2, early.rstd2, early.mean_e, early.minus_mean3, early.rstd3, early.offset3 = rings(
        ("mean2", "rstd2", "mean_e", "minus_mean3", "rstd3", "offset3"), 4, (NK,))
    early.graph = ring_of_four(nc, ctx, "graph", 4, (6, GB))
    return early


def late_buffers(nc, ctx):
    late = Parts()
    late.x3, late.y3, late.result = (ring_of_four(nc, ctx, name, 2) for name in ("x3", "y3", "result"))
    late.v_hi, late.v_lo, late.u2_hi, late.u2_lo, late.u1_hi, late.u1_lo = (
        ring_of_four(nc, ctx, name, 2, dt=F32R) for name in ("v_hi", "v_lo", "u2_hi", "u2_lo", "u1_hi", "u1_lo"))
    return late


def layers23(nc, psum, sem, early, late, h_new_set, x_store, h_store, out_dram, ident, adj_tr, adj_hi, adj_lo, cheb3,
             att_col, att_rep, consts, ones):
    U = 4
    x_in, h_in, x2, y2, h2, h3 = early.x_in, early.h_in, early.x2, early.y2, early.h2, early.h3
    scores, att, values, graph = early.scores, early.att, early.values, early.graph
    shift, top, nbias, sums, inv = early.shift, early.top, early.nbias, early.sums, early.inv
    stats2, work2, mean2, rstd2 = early.stats2, early.work2, early.mean2, early.rstd2
    stats3, work3, minus_mean3, rstd3, offset3 = early.stats3, early.work3, early.minus_mean3, early.rstd3, early.offset3
    stats_e, work_e, mean_e = early.stats_e, early.work_e, early.mean_e
    x3, y3, result = late.x3, late.y3, late.result
    v_hi, v_lo, u2_hi, u2_lo, u1_hi, u1_lo = late.v_hi, late.v_lo, late.u2_hi, late.u2_lo, late.u1_hi, late.u1_lo
    n2, ne, n3 = norm_sems(sem, "l2_n2"), norm_sems(sem, "l2_ne"), norm_sems(sem, "l3_n3")
    x_landed = [sem(f"l2_x_landed{k}") for k in range(U)]
    h_landed = [sem(f"l2_h_landed{k}") for k in range(U)]
    out_stored = [sem(f"l3_out_stored{k}") for k in range(U)]
    names = ("back", "x2_set", "y2_set", "turned2", "h2_set", "row_sum", "col_sum", "graph_sum", "graph_eps",
             "graph_root", "graph_set", "shift_set", "f_set", "leaky_set", "top_set", "nbias_set", "weights_set",
             "inv_set", "values_set", "att_sum", "att_set", "sig_set", "x3_set", "y3_set", "turned3", "h3_set",
             "v_sum", "v_hi_set", "v_lo_set", "u2_sum", "u2_hi_set", "u2_lo_set", "u1_sum", "u1_hi_set", "u1_lo_set",
             "o_sum", "result_set", "offset_set")
    (back, x2_set, y2_set, turned2, h2_set, row_sum, col_sum, graph_sum, graph_eps, graph_root, graph_set, shift_set,
     f_set, leaky_set, top_set, nbias_set, weights_set, inv_set, values_set, att_sum, att_set, sig_set, x3_set,
     y3_set, turned3, h3_set, v_sum, v_hi_set, v_lo_set, u2_sum, u2_hi_set, u2_lo_set, u1_sum, u1_hi_set,
     u1_lo_set, o_sum, result_set, offset_set) = (sem("l2_" + n) for n in names)
    TURN3, TURN2, O_BANK, ROW_J, BACK, U1_BANK, U2_BANK, ROW_I = (psum[:, k] for k in range(8))
    COL_J, ATT, V_BANK = ROW_J, BACK, TURN3

    def sync(sp):
        def body(stage):
            if i := stage(0):
                at = place(sp, i.index())
                wait(sp, x2_set, i.count(2))
                wait(sp, back, i.count(2))
                if isinstance(i.q, int):
                    sp.wait_ge(h_new_set, ITEMS - G + i.index() + 1)
                sp.dma_start(x_in[i.r], x_store[:, at]).then_inc(x_landed[i.r], 16)
                sp.dma_start(h_in[i.r], h_store[:, at]).then_inc(h_landed[i.r], 16)
            if i := stage(8):
                at = place(sp, i.index())
                sp.wait_ge(result_set, i.count())
                for b in range(GB):
                    sp.dma_start(out_dram[at * GB + b],
                                 result[i.r].rearrange("p (t b f) -> p b t f", t=NT, b=GB)[:, b]).then_inc(out_stored[i.r], 16)
        return Sweep(sp, G, U, 2, 8, body)

    def all_stored(sp):
        for k in range(U):
            sp.wait_ge(out_stored[k], 16 * GB * (G // U))

    def gpsimd(pool):
        def body(stage):
            if i := stage(2):
                k = i.r
                var = variance(pool, ne, i, stats_e[k], work_e[k], mean_e[k], N, 0.0, consts)
                mean_g, var_g, rs, root, lift, minus_rs = (graph[k][:, n, :] for n in range(6))
                pool.wait_ge(ne["var"], i.count())
                wait(pool, weights_set, i.count(4))
                pool.tensor_tensor(mean_g, mean_e[k][:, 0:GB], mean_e[k][:, GB:NK], ALU.add).then_inc(graph_sum, 1)
                pool.tensor_tensor(var_g, var[:, 0:GB], var[:, GB:NK], ALU.add).then_inc(graph_sum, 1)
                pool.wait_ge(graph_sum, i.count(per=2))
                pool.tensor_tensor(var_g, var_g, consts[:, EPS, 0:GB], ALU.add).then_inc(graph_eps, 1)
                pool.wait_ge(graph_eps, i.count())
                pool.tensor_tensor(rs, var_g, consts[:, MINUS_HALF, 0:GB], ALU.pow).then_inc(graph_root, 1)
                pool.tensor_tensor(root, var_g, consts[:, HALF, 0:GB], ALU.pow).then_inc(graph_root, 1)
                pool.wait_ge(graph_root, i.count(per=2))
                pool.tensor_tensor(lift, root, mean_g, ALU.subtract).then_inc(graph_set, 1)
                pool.tensor_scalar(minus_rs, rs, -1.0, 0.0, ALU.mult, ALU.add).then_inc(graph_set, 1)
            if i := stage(4):
                k = i.r
                wait(pool, y3_set, i.count(4))
                norm_scalars(pool, n3, i, stats3[k], work3[k], minus_mean3[k], rstd3[k], consts, half=-0.5)
                pool.wait_ge(n3["rstd"], i.count())
                pool.tensor_tensor(offset3[k], minus_mean3[k], rstd3[k], ALU.mult).then_inc(offset_set, 1)
            yield
            if i := stage(0):
                k = i.r
                wait(pool, y2_set, i.count(4))
                norm_scalars(pool, n2, i, stats2[k], work2[k], mean2[k], rstd2[k], consts)
            yield
            if i := stage(3):
                pool.wait_ge(att_set, i.count())
                pool.tensor_tensor(att[i.r], att[i.r], ones[:], ALU.add).then_inc(sig_set, 1)
        return Sweep(pool, G, U, 2, 4, body)

    def vector(dve):
        def low(i, hi_set, out_free, out, bank, hi, done):
            dve.wait_ge(hi_set, i.count())
            wait(dve, out_free, i.count(2))
            dve.tensor_tensor(out, bank, hi.bitcast(F32), ALU.subtract).then_inc(done, 1)

        def ahead(i):
            return isinstance(i.q, int) and i.index() < 3

        def x2_stats(i):
            dve.wait_ge(x2_set, i.count())
            wait(dve, n2["sums"], i.count(4, per=3))
            norm_stats(dve, n2, stats2[i.r], x2[i.r], D)

        def body(stage):
            if i := stage(6):
                low(i, u1_hi_set, o_sum, u1_lo[i.r], U1_BANK, u1_hi[i.r], u1_lo_set)
            if i := stage(1):
                k = i.r
                dve.wait_ge(n2["rstd"], i.count())
                wait(dve, turned2, i.count(4))
                wait(dve, values_set, i.count(4))
                normalise(dve, y2[k], x2[k], mean2[k], rstd2[k], y2_set)
            if i := stage(5):
                low(i, v_hi_set, u2_sum, v_lo[i.r], V_BANK, v_hi[i.r], v_lo_set)
            if i := stage(6):
                dve.wait_ge(o_sum, i.count())
                if before := i.before(2):
                    dve.wait_ge(out_stored[before.r], before.dma(GB))
                dve.tensor_tensor(result[i.r], O_BANK, x3[i.r], ALU.add).then_inc(result_set, 1)
            if i := stage(4):
                k = i.r
                dve.wait_ge(sig_set, i.count())
                wait(dve, y3_set, i.count(2))
                wait(dve, result_set, i.count(2))
                dve.scalar_tensor_tensor(x3[k], att[k], 0.5, x2[k], ALU.mult, ALU.add).then_inc(x3_set, 1)
                dve.wait_ge(x3_set, i.count())
                wait(dve, n3["sums"], i.count(4, per=3))
                norm_stats(dve, n3, stats3[k], x3[k], D)
            if i := stage(3):
                dve.wait_ge(weights_set, i.count())
                wait(dve, values_set, i.count(2))
                dve.reciprocal(inv[i.r], sums[i.r]).then_inc(inv_set, 1)
            yield
            if i := stage(0):
                k = i.r
                dve.wait_ge(back, i.count())
                dve.wait_ge(x_landed[k], i.dma())
                wait(dve, x3_set, i.count(4))
                dve.tensor_tensor(x2[k], BACK, x_in[k], ALU.add).then_inc(x2_set, 1)
                if ahead(i):
                    x2_stats(i)
            yield
            if i := stage(2):
                k = i.r
                dve.wait_ge(graph_set, i.count(per=2))
                dve.wait_ge(col_sum, i.count())
                wait(dve, f_set, i.count(2))
                for b in range(GB):
                    last = dve.tensor_scalar(shift[k][:, b * NT:(b + 1) * NT], COL_J[:, b * NT:(b + 1) * NT],
                                             graph[k][:, 4, b:b + 1], None, ALU.add)
                last.then_inc(shift_set, 1)
                dve.wait_ge(shift_set, i.count())
                wait(dve, att_sum, i.count(2))
                for b in range(GB):
                    for t in range(NT):
                        c = b * NT + t
                        last = dve.scalar_tensor_tensor(scores[k][:, c, :], ROW_I[:, b * N:(b + 1) * N],
                                                        shift[k][:, c:c + 1], adj_tr[:, t, :], ALU.add, ALU.mult)
                last.then_inc(f_set, 1)
            if (i := stage(0)) and not ahead(i):
                x2_stats(i)
            if i := stage(5):
                low(i, u2_hi_set, u1_sum, u2_lo[i.r], U2_BANK, u2_hi[i.r], u2_lo_set)
            if i := stage(2):
                k = i.r
                dve.wait_ge(f_set, i.count())
                dve.scalar_tensor_tensor(scores[k], scores[k], LEAK, scores[k], ALU.mult, ALU.max).then_inc(leaky_set, 1)
            if i := stage(2):
                k = i.r
                dve.wait_ge(leaky_set, i.count())
                wait(dve, nbias_set, i.count(2))
                dve.tensor_reduce(top[k], scores[k], AX.X, ALU.max).then_inc(top_set, 1)
                dve.wait_ge(top_set, i.count())
                wait(dve, weights_set, i.count(2))
                for b in range(GB):
                    last = dve.tensor_scalar(nbias[k][:, b * NT:(b + 1) * NT], top[k][:, b * NT:(b + 1) * NT],
                                             graph[k][:, 5, b:b + 1], None, ALU.mult)
                last.then_inc(nbias_set, 1)
            yield
            if i := stage(1):
                k = i.r
                dve.wait_ge(row_sum, i.count())
                wait(dve, ne["sums"], i.count(4, per=3))
                for b in range(GB):
                    dve.bn_stats(stats_e[k][:, b, :], ROW_I[:, b * N:(b + 1) * N])
                for b in range(GB):
                    last = dve.bn_stats(stats_e[k][:, GB + b, :], ROW_J[:, b * N:(b + 1) * N])
                last.then_inc(ne["stats"], 1)
        return Sweep(dve, G, U, 2, 6, body)

    def scalar(act):
        def high(i, summed, out_free, out, bank, done):
            act.wait_ge(summed, i.count())
            wait(act, out_free, i.count(2))
            act.activation(out, bank, ACT.Copy).then_inc(done, 1)

        def body(stage):
            if i := stage(2):
                k = i.r
                act.wait_ge(inv_set, i.count())
                wait(act, att_sum, i.count(2))
                for t in range(NT):
                    for b in range(GB):
                        n, c = t * GB + b, b * NT + t
                        last = act.activation(values[k][:, n * D:(n + 1) * D], y2[k][:, n * D:(n + 1) * D],
                                              ACT.Relu, scale=inv[k][:, c:c + 1])
                last.then_inc(values_set, 1)
            if i := stage(4):
                high(i, u2_sum, u1_sum, u2_hi[i.r], U2_BANK, u2_hi_set)
            if i := stage(0):
                act.wait_ge(turned2, i.count())
                wait(act, col_sum, i.count(4))
                act.activation(h2[i.r], TURN2, ACT.Relu).then_inc(h2_set, 1)
            if i := stage(3):
                k = i.r
                act.wait_ge(offset_set, i.count())
                wait(act, turned3, i.count(2))
                for n in range(NK):
                    last = act.activation(y3[k][:, n * D:(n + 1) * D], x3[k][:, n * D:(n + 1) * D], ACT.Identity,
                                          bias=offset3[k][:, n:n + 1], scale=rstd3[k][:, n:n + 1])
                last.then_inc(y3_set, 1)
            if i := stage(2):
                act.wait_ge(att_sum, i.count())
                wait(act, x3_set, i.count(2))
                act.activation(att[i.r], ATT, ACT.Tanh, scale=0.5).then_inc(att_set, 1)
            if i := stage(4):
                high(i, u1_sum, o_sum, u1_hi[i.r], U1_BANK, u1_hi_set)
            if i := stage(3):
                act.wait_ge(turned3, i.count())
                wait(act, o_sum, i.count(2))
                act.activation(h3[i.r], TURN3, ACT.Relu).then_inc(h3_set, 1)
            if i := stage(3):
                high(i, v_sum, u2_sum, v_hi[i.r], V_BANK, v_hi_set)
            yield
            if i := stage(1):
                k = i.r
                act.wait_ge(nbias_set, i.count())
                wait(act, inv_set, i.count(2))
                for c in range(NK):
                    last = act.activation(scores[k][:, c, :], scores[k][:, c, :], ACT.Exp, bias=nbias[k][:, c:c + 1],
                                          scale=graph[k][:, 2, c // NT:c // NT + 1], accum_out=sums[k][:, c:c + 1])
                last.then_inc(weights_set, 1)
        return Sweep(act, G, U, 2, 4, body)

    def tensor(pe):
        def body(stage):
            if i := stage(0):
                pe.wait_ge(h_landed[i.r], i.dma())
                wait(pe, x2_set, i.count(1))
                wait(pe, att_set, i.count(4))
                flip_back(pe, BACK, h_in[i.r], ident, back)
            if i := stage(5):
                pe.wait_ge(h3_set, i.count())
                by_weight(pe, V_BANK, h3[i.r], cheb3[:, 3, :]).then_inc(v_sum, 1)
            if i := stage(6):
                pe.wait_ge(u1_lo_set, i.count())
                by_adjacency(pe, O_BANK, adj_hi, adj_lo, u1_hi[i.r], u1_lo[i.r]).then_inc(o_sum, 1)
            yield
            if i := stage(1):
                pe.wait_ge(y2_set, i.count())
                wait(pe, h2_set, i.count(1))
                flip(pe, TURN2, y2[i.r], ident, turned2)
            if i := stage(5):
                wait(pe, u2_lo_set, i.count(1))
                by_weight(pe, U2_BANK, h3[i.r], cheb3[:, 2, :])
            yield
            if i := stage(2):
                pe.wait_ge(ne["stats"], i.count())
                for c in range(NK):
                    last = pe.matmul(COL_J[:, c:c + 1], h2[i.r][:, c * P:(c + 1) * P], att_col[:, 1:2],
                                     start=(c == 0), stop=False, skip_group_check=True)
                last.then_inc(col_sum, 1)
            yield
            if i := stage(5):
                pe.wait_ge(v_lo_set, i.count())
                by_adjacency(pe, U2_BANK, adj_hi, adj_lo, v_hi[i.r], v_lo[i.r]).then_inc(u2_sum, 1)
                wait(pe, u1_lo_set, i.count(1))
                by_weight(pe, U1_BANK, h3[i.r], cheb3[:, 1, :])
            if i := stage(3):
                k = i.r
                pe.wait_ge(values_set, i.count())
                pe.wait_ge(x2_set, i.count(-3))
                first = True
                for t in range(NT):
                    for b in range(GB):
                        n = t * GB + b
                        for j in range(NT):
                            last = pe.matmul(ATT[:, n * D:(n + 1) * D], scores[k][:, b * NT + j, t * P:(t + 1) * P],
                                             values[k][:, (j * GB + b) * D:(j * GB + b + 1) * D],
                                             start=first, stop=False, skip_group_check=True)
                            first = False
                last.then_inc(att_sum, 1)
            yield
            if i := stage(1):
                k = i.r
                pe.wait_ge(h2_set, i.count())
                wait(pe, f_set, i.count(1))
                pe.matmul(ROW_I, att_rep[:, 0, :], h2[k], start=True, stop=True)
                wait(pe, shift_set, i.count(1))
                pe.matmul(ROW_J, att_rep[:, 1, :], h2[k], start=True, stop=True).then_inc(row_sum, 1)
            if i := stage(5):
                pe.wait_ge(u2_lo_set, i.count())
                by_adjacency(pe, U1_BANK, adj_hi, adj_lo, u2_hi[i.r], u2_lo[i.r]).then_inc(u1_sum, 1)
            if i := stage(4):
                pe.wait_ge(y3_set, i.count())
                wait(pe, v_lo_set, i.count(1))
                flip(pe, TURN3, y3[i.r], ident, turned3)
            if i := stage(5):
                wait(pe, result_set, i.count(1))
                by_weight(pe, O_BANK, h3[i.r], cheb3[:, 0, :])
        return Sweep(pe, G, U, 2, 6, body)

    parts = Parts()
    parts.sync, parts.gpsimd, parts.vector, parts.scalar, parts.tensor = sync, gpsimd, vector, scalar, tensor
    parts.all_stored = all_stored
    return parts


_INS = ['x', 'adj', 'L0_gnn_Theta1', 'L0_gnn_bias', 'L1_gnn_w3_w', 'L1_gnn_w3_b', 'L1_gnn_u3_w', 'L1_gnn_u3_b',
        'L1_gnn_w4_w', 'L1_gnn_w4_b', 'L1_gnn_w5_w', 'L1_gnn_w5_b', 'L1_gnn_u5_w', 'L1_gnn_u5_b', 'L2_gnn_a',
        'L3_gnn_weight_1']
_OUTS = [((B, N, D), 'float32')]


def kernel(**inputs):
    import numpy as _np
    import concourse.bacc as _bacc
    from concourse import mybir as _mybir
    from concourse.bass_utils import run_bass_kernel_spmd as _run

    nc = _bacc.Bacc("TRN2", target_bir_lowering=False, num_devices=1)
    arrays, args = {}, []
    for name in _INS:
        a = _np.ascontiguousarray(inputs[name])
        arrays[f"in_{name}_dram"] = a
        args.append(nc.dram_tensor(f"in_{name}_dram", a.shape, _mybir.dt.from_np(a.dtype), kind="ExternalInput").ap())
    for i, (shape, dtype) in enumerate(_OUTS):
        dt = _mybir.dt.from_np(_np.dtype(dtype))
        args.append(nc.dram_tensor(f"out_{i}_dram", shape, dt, kind="ExternalOutput").ap())
    build(nc, *args)
    r = _run(nc, [arrays], core_ids=[0])
    return r.results[0]["out_0_dram"]
```
